# Optimizing a Trainium2 kernel written in Bass

```python
import numpy as np
import jax
import jax.numpy as jnp

def _softmax(x, axis=-1):
    return jax.nn.softmax(x, axis=axis)

def _gelu(x):
    return jax.nn.gelu(x, approximate=True)

def _silu(x):
    return jax.nn.silu(x)

def _sigmoid(x):
    return jax.nn.sigmoid(x)

def _layernorm(x, axis=-1, eps=1e-05):
    m = jnp.mean(x, axis=axis, keepdims=True)
    v = jnp.var(x, axis=axis, keepdims=True)
    return (x - m) / jnp.sqrt(v + eps)

def _scatter_add(tgt, idx, src, axis=0):
    return tgt.at[idx].add(src)

def _segment_sum(src, seg, n):
    return jax.ops.segment_sum(src, seg, n)
kernel_name = 'mk_adj_seq_d1_adj_r2_a7f8b7'

def setup_inputs(seed: int=0):
    np.random.seed(seed)
    _w = jnp.asarray

    def _rec_inputs():
        import jax
        import jax.numpy as jnp
        _gk = jax.random.key(seed)
        x = -0.0002928 + 1 * jax.random.normal(jax.random.fold_in(_gk, 1), (8, 1024, 256), jnp.float32)
        _w = (1.0 + jnp.arange(1024, dtype=jnp.float32)) ** (-0.5)
        _w = _w / _w.mean()
        _pij = jnp.clip(0.015625 * _w[:, None] * _w[None, :], 0.0, 1.0)
        _a = jax.random.uniform(jax.random.fold_in(_gk, 2), (8, 1024, 1024)) < _pij
        _a = jnp.logical_or(_a, jnp.swapaxes(_a, -1, -2))
        _a = jnp.logical_or(_a, jnp.eye(1024, dtype=bool))
        _af = _a.astype(jnp.float32)
        _af = _af / jnp.maximum(_af.sum(-1, keepdims=True), 1.0)
        adj = _af
        return (x, adj)
    x, adj = _rec_inputs()

    def _L0_gnn_setup():
        import jax, jax.numpy as jnp
        import numpy as np
        B, N, D, H = (8, 512, 256, 8)
        DK = D // H
        LN_EPS = 1e-05
        ADJ_MIN = 1e-08

        def _layer_norm(x, gamma, beta):
            mu = jnp.mean(x, axis=-1, keepdims=True)
            var = jnp.mean(jnp.square(x - mu), axis=-1, keepdims=True)
            return (x - mu) * jax.lax.rsqrt(var + LN_EPS) * gamma + beta
        key = jax.random.key(seed)
        ks = jax.random.split(key, 12)
        x = jax.random.normal(ks[0], (B, N, D), dtype=jnp.float32)
        adj = jax.random.uniform(ks[1], (B, N, N), dtype=jnp.float32)
        adj = adj / jnp.sum(adj, axis=-1, keepdims=True)
        s = 1.0 / np.sqrt(D)
        Wq = jax.random.normal(ks[2], (D, D), dtype=jnp.float32) * s
        bq = jnp.zeros((D,), dtype=jnp.float32)
        Wk = jax.random.normal(ks[3], (D, D), dtype=jnp.float32) * s
        bk = jnp.zeros((D,), dtype=jnp.float32)
        Wv = jax.random.normal(ks[4], (D, D), dtype=jnp.float32) * s
        bv = jnp.zeros((D,), dtype=jnp.float32)
        Wo = jax.random.normal(ks[5], (D, D), dtype=jnp.float32) * s
        bo = jnp.zeros((D,), dtype=jnp.float32)
        gamma = jnp.ones((D,), dtype=jnp.float32)
        beta = jnp.zeros((D,), dtype=jnp.float32)
        return {'x': x, 'adj': adj, 'Wq': Wq, 'bq': bq, 'Wk': Wk, 'bk': bk, 'Wv': Wv, 'bv': bv, 'Wo': Wo, 'bo': bo, 'gamma': gamma, 'beta': beta}
    _L0_gnn_all = _L0_gnn_setup()
    _L0_gnn_in = {k: v for k, v in _L0_gnn_all.items() if k in ('Wq', 'bq', 'Wk', 'bk', 'Wv', 'bv', 'Wo', 'bo', 'gamma', 'beta')}
    del _L0_gnn_all
    return {'x': x, 'adj': adj, 'L0_gnn_Wq': _L0_gnn_in['Wq'], 'L0_gnn_bq': _L0_gnn_in['bq'], 'L0_gnn_Wk': _L0_gnn_in['Wk'], 'L0_gnn_bk': _L0_gnn_in['bk'], 'L0_gnn_Wv': _L0_gnn_in['Wv'], 'L0_gnn_bv': _L0_gnn_in['bv'], 'L0_gnn_Wo': _L0_gnn_in['Wo'], 'L0_gnn_bo': _L0_gnn_in['bo'], 'L0_gnn_gamma': _L0_gnn_in['gamma'], 'L0_gnn_beta': _L0_gnn_in['beta']}

def reference(x, adj, L0_gnn_Wq, L0_gnn_bq, L0_gnn_Wk, L0_gnn_bk, L0_gnn_Wv, L0_gnn_bv, L0_gnn_Wo, L0_gnn_bo, L0_gnn_gamma, L0_gnn_beta):
    import jax
    import jax.numpy as jnp

    def _L0_gnn_ref(x, adj, Wq, bq, Wk, bk, Wv, bv, Wo, bo, gamma, beta):
        import jax, jax.numpy as jnp
        import numpy as np
        B, N, D, H = (8, 512, 256, 8)
        DK = D // H
        LN_EPS = 1e-05
        ADJ_MIN = 1e-08

        def _layer_norm(x, gamma, beta):
            mu = jnp.mean(x, axis=-1, keepdims=True)
            var = jnp.mean(jnp.square(x - mu), axis=-1, keepdims=True)
            return (x - mu) * jax.lax.rsqrt(var + LN_EPS) * gamma + beta
        b, n, d = x.shape
        q = (x @ Wq.T + bq).reshape(b, n, H, DK).transpose(0, 2, 1, 3)
        k = (x @ Wk.T + bk).reshape(b, n, H, DK).transpose(0, 2, 1, 3)
        v = (x @ Wv.T + bv).reshape(b, n, H, DK).transpose(0, 2, 1, 3)
        logits = jnp.einsum('bhqd,bhkd->bhqk', q, k) / np.sqrt(DK)
        logits = logits + jnp.log(jnp.clip(adj, ADJ_MIN, None))[:, None, :, :]
        attn = jax.nn.softmax(logits, axis=-1)
        out = jnp.einsum('bhqk,bhkd->bhqd', attn, v)
        out = out.transpose(0, 2, 1, 3).reshape(b, n, d)
        out = out @ Wo.T + bo
        return _layer_norm(x + out, gamma, beta)
    x = _L0_gnn_ref(x, adj, L0_gnn_Wq, L0_gnn_bq, L0_gnn_Wk, L0_gnn_bk, L0_gnn_Wv, L0_gnn_bv, L0_gnn_Wo, L0_gnn_bo, L0_gnn_gamma, L0_gnn_beta)
    return x

_drawn_inputs = setup_inputs


def setup_inputs(seed=0):
    import zlib

    import numpy as np

    out = dict(_drawn_inputs(seed))
    spreads = {'L0_gnn_bq': (0.0, 0.322),
     'L0_gnn_bk': (0.0, 0.8),
     'L0_gnn_bv': (0.0, 0.1),
     'L0_gnn_bo': (0.0, 0.1),
     'L0_gnn_gamma': (1.0, 0.2),
     'L0_gnn_beta': (0.0, 0.1)}
    factors = {}
    for name, (base, spread) in spreads.items():
        noise = np.random.default_rng([zlib.crc32(name.encode()), seed]).standard_normal(out[name].shape)
        drawn = base * np.exp(spread * noise) if base else spread * noise
        out[name] = jnp.asarray(drawn.astype(out[name].dtype))
    for name, factor in factors.items():
        out[name] = (out[name] * factor).astype(out[name].dtype)
    return out
```

```python
from contextlib import ExitStack

import concourse.bass as bass
from concourse import mybir

F32 = mybir.dt.float32
F32R = mybir.dt.float32r
ALU = mybir.AluOpType
ACT = mybir.ActivationFunctionType

P = 128
B, N, D, H = 8, 1024, 256, 8
DK = D // H
DC = D // P
SCALE = float(DK) ** -0.5
LN_EPS = 1e-05
ADJ_MIN = 1e-08
NEVER = 3.0e38

HALVES = 2
TOK = N // HALVES
TT = TOK // P
OUTS = 6

QT = 2
PAIR = QT * P
PAIRS = B * N // PAIR
PPB = N // PAIR
UNITS = H * QT
QUADS = 2
QH = H // QUADS
KT = N // P
HK = KT // 2
AHEAD = 2
LSLOTS = 4
GROUPS = P // DK

K_PART = [0, 1, 0, 1]
Q_PART = [0, 0, 1, 1]

PV_STEPS = {2: (0,), 3: (1, 2), 4: (3,), 5: (4, 5), 6: (6, 7)}
R_STEP = 7
OUT_STEP = 10

RING = 3
USES = []
for _j in range(UNITS):
    if _j == OUT_STEP:
        USES.append(("out", 0))
    USES += [("a", _j), ("b", _j)]
assert len(USES) % RING == 0
SCALAR_TAKES_A = (6, 14)


def unit(j):
    return 2 * (j // 4) + j % 2, (j % 4) // 2


def evacuator(use):
    kind, j = use
    return "vector" if kind == "out" or (kind == "a" and j not in SCALAR_TAKES_A) else "scalar"


def evacuated(use, engine):
    return sum(evacuator(x) == engine and x[0] != "out" for x in USES[:USES.index(use) + 1])


VECTOR_EVACS = evacuated(USES[-1], "vector")
SCALAR_EVACS = evacuated(USES[-1], "scalar")


def graph_attention(nc, x, xT, adj, wqT, wkT, wvT, woT, bq, bk, bv, bo, gamma, beta, out):
    x_rows = x.rearrange("b t d -> (b t) d")
    adj_rows = adj.rearrange("b q k -> (b q) k")
    out_rows = out.rearrange("b t d -> (b t) d")
    q_dram = nc.dram_tensor("q_parts", (2 * D, B * N), F32, kind="Internal").ap()
    k_dram = nc.dram_tensor("k_parts", (2 * D, B * N), F32, kind="Internal").ap()
    v_dram = nc.dram_tensor("v_scratch", (B * N, D), F32, kind="Internal").ap()
    q_store = q_dram.rearrange("(l m p) t -> p m l t", l=2, m=DC)
    k_store = k_dram.rearrange("(l m p) t -> p m l t", l=2, m=DC)

    with ExitStack() as ctx:
        def sb(name, shape, dt=F32, scope=ctx):
            return scope.enter_context(nc.sbuf_tensor(name, shape, dt))

        def sem(name):
            return ctx.enter_context(nc.semaphore(name))

        ident = sb("ident", [P, P])
        bq_col = sb("bq_col", [P, DC])
        bqs_col = sb("bqs_col", [P, DC])
        bk_col = sb("bk_col", [P, DC])
        bv_row = sb("bv_row", [P, D])
        bo_row = sb("bo_row", [P, D])
        gamma_row = sb("gamma_row", [P, D])
        beta_row = sb("beta_row", [P, D])
        wo = sb("wo", [P, DC, D])
        minus_half = sb("minus_half", [P, QT])
        k_stack = sb("k_stack", [P, H, N], F32R)
        q_stack = [sb(f"q_stack{q}", [P, QH, PAIR], F32R) for q in range(QUADS)]
        v_sb = sb("v_sb", [P, KT, D])
        adj_in = [sb(f"adj_in{t}", [P, N]) for t in range(QT)]
        log_adj = [sb(f"log_adj{t}", [P, N]) for t in range(QT)]
        neg_logits = [sb(f"neg_logits{s}", [P, N]) for s in range(LSLOTS)]
        neg_max = [sb(f"neg_max{s}", [P, 1]) for s in range(LSLOTS)]
        probs = [sb(f"probs{s}", [P, N]) for s in range(2)]
        row_sum = [sb(f"row_sum{q}", [P, QT, QH]) for q in range(QUADS)]
        inv_sum = [sb(f"inv_sum{q}", [P, QT, QH]) for q in range(QUADS)]
        inv_wide = [sb(f"inv_wide{q}", [P, QT, QH, DK]) for q in range(QUADS)]
        inv_bcast = sb("inv_bcast", [P, PAIR])
        attn_T = [sb(f"attn_T{q}", [P, PAIR]) for q in range(QUADS)]
        x_bo = sb("x_bo", [P, QT, D])
        resid = sb("resid", [P, QT, D])
        stats = sb("stats", [P, QT, 6])
        mean_var = sb("mean_var", [P, QT, 2])
        rstd = sb("rstd", [P, 2, QT])
        normed = sb("normed", [P, QT, D])

        with ExitStack() as early:
            w_raw = [sb(f"w_raw{i}", [P, DC, D], F32, early) for i in range(3)]
            w_hi = [sb(f"w_hi{i}", [P, DC, D], F32R, early) for i in range(3)]
            w_lo = [sb(f"w_lo{i}", [P, DC, D], F32R, early) for i in range(3)]
            xT_in = [sb(f"xT_in{h}", [P, DC, TOK], F32, early) for h in range(HALVES)]
            x_hi = [sb(f"x_hi{h}", [P, DC, TOK], F32R, early) for h in range(HALVES)]
            x_lo = [sb(f"x_lo{h}", [P, DC, TOK], F32R, early) for h in range(HALVES)]
            k_out = [sb(f"k_out{h}", [P, DC, 2, TOK], F32R, early) for h in range(HALVES)]
            q_out = [sb(f"q_out{h}", [P, DC, 2, TOK], F32R, early) for h in range(HALVES)]
            v_out = [sb(f"v_out{h}", [P, TT, D], F32, early) for h in range(HALVES)]
        probs_T = [sb(f"probs_T{q}", [P, QH, KT, PAIR]) for q in range(QUADS)]

        with nc.psum_tensor("proj", [P, OUTS, TOK], F32) as proj:
            pass
        score = [ctx.enter_context(nc.psum_tensor(f"score{s}", [P, N], F32)) for s in range(2)]
        ring = [ctx.enter_context(nc.psum_tensor(f"ring{s}", [P, TOK], F32)) for s in range(RING)]
        attn = ctx.enter_context(nc.psum_tensor("attn", [P, 2, PAIR], F32))

        weights_in = sem("weights_in")
        consts_in = sem("consts_in")
        ident_ready = sem("ident_ready")
        bias_scaled = sem("bias_scaled")
        w_hi_ready = sem("w_hi_ready")
        w_lo_ready = sem("w_lo_ready")
        xT_loaded = [sem(f"xT_loaded{h}") for h in range(HALVES)]
        x_hi_ready = sem("x_hi_ready")
        x_lo_ready = sem("x_lo_ready")
        proj_ready = sem("proj_ready")
        proj_hi_done = sem("proj_hi_done")
        proj_done = sem("proj_done")
        stored = [sem(f"stored{h}") for h in range(HALVES)]

        k_loaded = [sem(f"k_loaded{i}") for i in range(H // 2)]
        q_loaded = [sem(f"q_loaded{q}") for q in range(QUADS)]
        v_loaded = sem("v_loaded")
        adj_loaded = [sem(f"adj_loaded{t}") for t in range(QT)]
        x_loaded = sem("x_loaded")
        adj_clipped = sem("adj_clipped")
        log_adj_ready = sem("log_adj_ready")
        scores_ready = sem("scores_ready")
        logits_ready = sem("logits_ready")
        probs_ready = sem("probs_ready")
        half_a_ready = sem("half_a_ready")
        half_b_ready = sem("half_b_ready")
        vector_evac = sem("vector_evac")
        scalar_evac = sem("scalar_evac")
        inv_ready = sem("inv_ready")
        inv_widened = sem("inv_widened")
        pv_done = sem("pv_done")
        bcast_ready = sem("bcast_ready")
        bcast_copied = sem("bcast_copied")
        attn_ready = sem("attn_ready")
        out_proj_ready = sem("out_proj_ready")
        x_bo_ready = sem("x_bo_ready")
        resid_ready = sem("resid_ready")
        bn_step = sem("bn_step")
        stats_ready = sem("stats_ready")
        ln_step = sem("ln_step")
        normed_ready = sem("normed_ready")
        out_stored = sem("out_stored")

        def over_steps(eng, body):
            body(0, True, False)
            with eng.Fori(1, B - 1) as b:
                body(b, False, False)
            body(B - 1, False, True)

        def over_pairs(eng, body):
            body(0, False, True, True)
            with eng.Fori(1, PAIRS - 1) as g:
                body(g, True, True, True)
            body(PAIRS - 1, True, True, False)
            body(PAIRS, True, False, False)

        def at(eng, value):
            return value if isinstance(value, int) else eng.to_reg(value)

        block = ctx.enter_context(nc.Block())

        @block.sync
        def _(sp):
            for i, w in enumerate((wkT, wqT, wvT)):
                sp.dma_start(w_raw[i][:], w.rearrange("(c p) n -> p c n", p=P)).then_inc(weights_in, 16)

            def load_xT(b, h):
                sp.dma_start(xT_in[h][:], xT.rearrange("b (c p) t -> p b c t", p=P)
                             [:, bass.ds(b, 1), :, h * TOK:(h + 1) * TOK].rearrange("p o c t -> p (o c) t")).then_inc(xT_loaded[h], 16)

            for h in range(HALVES):
                load_xT(0, h)
            sp.dma_start(bq_col[:], bq).then_inc(consts_in, 16)
            sp.dma_start(bk_col[:], bk).then_inc(consts_in, 16)
            for row, vec in ((bv_row, bv), (bo_row, bo), (gamma_row, gamma), (beta_row, beta)):
                sp.dma_start(row[:], vec.partition_broadcast(P)).then_inc(consts_in, 16)
            sp.dma_start(wo[:], woT.rearrange("(c p) n -> p c n", p=P)).then_inc(consts_in, 16)

            def load_k(i, b):
                for gr in range(GROUPS):
                    row = K_PART[gr] * D + 2 * i * DK
                    sp.dma_start(k_stack[gr * DK:(gr + 1) * DK, 2 * i:2 * i + 2, :].bitcast(F32),
                                 k_dram[row:row + 2 * DK, bass.ds(b * N, N)]
                                 .rearrange("(h d) t -> d h t", h=2)).then_inc(k_loaded[i], 16)

            def load_q(q, g):
                for gr in range(GROUPS):
                    row = Q_PART[gr] * D + q * P
                    sp.dma_start(q_stack[q][gr * DK:(gr + 1) * DK, :, :].bitcast(F32),
                                 q_dram[row:row + P, bass.ds(g * PAIR, PAIR)]
                                 .rearrange("(h d) t -> d h t", h=QH)).then_inc(q_loaded[q], 16)

            def load_v(b):
                sp.dma_start(v_sb[:], v_dram[bass.ds(b * N, N), :]
                             .rearrange("(k p) d -> p k d", p=P)).then_inc(v_loaded, 16)

            def load_adj(t, g):
                sp.dma_start(adj_in[t][:], adj_rows[bass.ds(g * PAIR + t * P, P), :]).then_inc(adj_loaded[t], 16)

            def first_loads():
                for h in range(HALVES):
                    sp.wait_ge(stored[h], 16 * 5)
                for t in range(QT):
                    load_adj(t, 0)
                load_k(0, 0)
                load_q(0, 0)
                for i in range(1, H // 2):
                    load_k(i, 0)
                load_q(1, 0)
                load_v(0)

            def project(b, first, last):
                if last:
                    first_loads()
                for h in range(HALVES):
                    n = HALVES * b + h
                    if not last:
                        count = at(sp, n + 1)
                        sp.wait_ge(weights_in, 16 * 3)
                        sp.wait_ge(x_hi_ready, count)
                        sp.wait_ge(x_lo_ready, n + 1)
                        load_xT(b + 1, h)
                    for dst, src, done in ((k_store, k_out[h], 2), (q_store, q_out[h], 4)):
                        count = at(sp, OUTS * n + done)
                        sp.wait_ge(weights_in, 16 * 3)
                        sp.wait_ge(proj_done, count)
                        for m in range(DC):
                            sp.dma_start(dst[:, m, :, bass.ds(n * TOK, TOK)], src[:, m].bitcast(F32)).then_inc(stored[h], 16)
                    count = at(sp, OUTS * n + OUTS)
                    sp.wait_ge(weights_in, 16 * 3)
                    sp.wait_ge(proj_done, count)
                    sp.dma_start(v_dram[bass.ds(n * TOK, TOK), :].rearrange("(k p) d -> p k d", p=P),
                                 v_out[h][:]).then_inc(stored[h], 16)

            over_steps(sp, project)

            for h in range(HALVES):
                sp.wait_ge(stored[h], 16 * 5 * B)
            for t in range(QT):
                count = at(sp, t + 1)
                sp.wait_ge(weights_in, 16 * 3)
                sp.wait_ge(log_adj_ready, count)
                load_adj(t, 1)

            def attend(g, batch, new_batch, last_of_batch, more, more_adj):
                if last_of_batch and more:
                    count = at(sp, UNITS * g + 4)
                    sp.wait_ge(weights_in, 16 * 3)
                    sp.wait_ge(scores_ready, count)
                    load_k(0, batch + 1)
                if more:
                    count = at(sp, UNITS * g + 8)
                    sp.wait_ge(weights_in, 16 * 3)
                    sp.wait_ge(scores_ready, count)
                    load_q(0, g + 1)
                    if last_of_batch:
                        load_k(1, batch + 1)
                if new_batch:
                    count = at(sp, QUADS * g)
                    sp.wait_ge(weights_in, 16 * 3)
                    sp.wait_ge(pv_done, count)
                    load_v(batch)
                if last_of_batch and more:
                    count = at(sp, UNITS * g + 12)
                    sp.wait_ge(weights_in, 16 * 3)
                    sp.wait_ge(scores_ready, count)
                    load_k(2, batch + 1)
                if not (isinstance(g, int) and g == 0):
                    count = at(sp, g)
                    sp.wait_ge(weights_in, 16 * 3)
                    sp.wait_ge(resid_ready, count)
                sp.dma_start(x_bo[:], x_rows[bass.ds(g * PAIR, PAIR), :]
                             .rearrange("(s p) d -> p s d", p=P)).then_inc(x_loaded, 16)
                if more:
                    count = at(sp, UNITS * g + 16)
                    sp.wait_ge(weights_in, 16 * 3)
                    sp.wait_ge(scores_ready, count)
                    load_q(1, g + 1)
                    if last_of_batch:
                        load_k(3, batch + 1)
                if more_adj:
                    for t in range(QT):
                        count = at(sp, QT * g + QT + t + 1)
                        sp.wait_ge(weights_in, 16 * 3)
                        sp.wait_ge(log_adj_ready, count)
                        load_adj(t, g + 2)
                if not (isinstance(g, int) and g == 0):
                    store_out(g - 1)

            def store_out(g):
                count = at(sp, g + 1)
                sp.wait_ge(weights_in, 16 * 3)
                sp.wait_ge(normed_ready, count)
                sp.dma_start(out_rows[bass.ds(g * PAIR, PAIR), :].rearrange("(s p) d -> p s d", p=P),
                             normed[:]).then_inc(out_stored, 16)

            def batch_of_pairs(b, first, last):
                g = PPB * b
                attend(g, b, not first, False, True, True)
                attend(g + 1, b, False, False, True, True)
                attend(g + 2, b, False, False, True, not last)
                attend(g + 3, b, False, True, not last, not last)

            over_steps(sp, batch_of_pairs)
            store_out(PAIRS - 1)
            sp.wait_ge(out_stored, 16 * PAIRS)

        @block.tensor
        def _(pe):
            pe.wait_ge(w_hi_ready, 3)
            pe.wait_ge(w_lo_ready, 3)

            def project(b, first, last):
                for h in range(HALVES):
                    n = HALVES * b + h
                    pe.wait_ge(x_hi_ready, n + 1)
                    pe.wait_ge(x_lo_ready, n + 1)
                    for i, w in ((0, 0), (1, 0), (2, 1), (3, 1)):
                        if not (first and h == 0):
                            pe.wait_ge(proj_done, OUTS * (n - 1) + i + 1)
                        m = i % DC
                        terms = [(wp, xp, c) for c in range(DC)
                                 for wp, xp in ((w_hi, x_hi), (w_hi, x_lo), (w_lo, x_hi))]
                        for s, (wp, xp, c) in enumerate(terms):
                            mm = nc.tensor.matmul(proj[:, i, :], wp[w][:, c, m * P:(m + 1) * P], xp[h][:, c, :],
                                                  start=(s == 0), stop=(s == len(terms) - 1))
                        mm.then_inc(proj_ready, 1)
                    for i in (4, 5):
                        if not (first and h == 0):
                            pe.wait_ge(proj_done, OUTS * (n - 1) + i + 1)
                        for half in range(2):
                            t = 2 * (i - 4) + half
                            terms = [(xp, wp, c) for c in range(DC)
                                     for xp, wp in ((x_hi, w_hi), (x_lo, w_hi), (x_hi, w_lo))]
                            for s, (xp, wp, c) in enumerate(terms):
                                mm = nc.tensor.matmul(proj[:, i, half * D:(half + 1) * D],
                                                      xp[h][:, c, t * P:(t + 1) * P], wp[2][:, c, :],
                                                      start=(s == 0), stop=(s == len(terms) - 1))
                        mm.then_inc(proj_ready, 1)

            over_steps(pe, project)

            pe.wait_ge(proj_done, OUTS * HALVES * B)
            pe.wait_ge(ident_ready, 1)
            pe.wait_ge(consts_in, 16 * 7)

            def scores(g, j, first):
                head, t = unit(j)
                quad = j // 8
                if j % 8 == 0:
                    pe.wait_ge(q_loaded[quad], 16 * GROUPS * (g + 1))
                if j % 4 == 0:
                    pe.wait_ge(k_loaded[j // 4], 16 * GROUPS * ((g >> 2) + 1))
                if not (first and j < 2):
                    pe.wait_ge(logits_ready, UNITS * g + j - 1)
                for n in range(2):
                    mm = nc.tensor.matmul(score[j % 2][:, n * TOK:(n + 1) * TOK],
                                          q_stack[quad][:, head % QH, t * P:(t + 1) * P],
                                          k_stack[:, head, n * TOK:(n + 1) * TOK], start=True, stop=True)
                mm.then_inc(scores_ready, 1)

            def ring_free(g, use, first):
                i = USES.index(use)
                before = USES[(i - RING) % len(USES)]
                pairs_back = 1 if i < RING else 0
                if first and (pairs_back or before[0] == "out"):
                    return
                if before[0] == "out":
                    pe.wait_ge(resid_ready, g)
                elif evacuator(before) == "vector":
                    pe.wait_ge(vector_evac, VECTOR_EVACS * (g - pairs_back) + evacuated(before, "vector"))
                else:
                    pe.wait_ge(scalar_evac, SCALAR_EVACS * (g - pairs_back) + evacuated(before, "scalar"))

            def transposes(g, j, half, first):
                use = ("ab"[half], j)
                ring_free(g, use, first)
                bank = ring[USES.index(use) % RING]
                for k in range(HK):
                    kt = half * HK + k
                    mm = nc.tensor.transpose(bank[:, k * P:(k + 1) * P],
                                             probs[j % 2][:, kt * P:(kt + 1) * P], ident[:])
                mm.then_inc(half_b_ready if half else half_a_ready, 1)

            def values(g, quad, kts, first):
                if kts[0] == 0:
                    last = ("b", 8 * quad + 7)
                    pe.wait_ge(vector_evac, VECTOR_EVACS * g + evacuated(last, "vector"))
                    pe.wait_ge(scalar_evac, SCALAR_EVACS * g + evacuated(last, "scalar"))
                    pe.wait_ge(v_loaded, 16 * ((g >> 2) + 1))
                    if not (first and quad == 0):
                        pe.wait_ge(attn_ready, QUADS * g + quad)
                for kt in kts:
                    for hh in range(QH):
                        head = QH * quad + hh
                        mm = nc.tensor.matmul(attn[hh * DK:(hh + 1) * DK, 0, :],
                                              v_sb[:, kt, head * DK:(head + 1) * DK],
                                              probs_T[quad][:, hh, kt, :], start=(kt == 0), stop=(kt == KT - 1))
                if kts[-1] == KT - 1:
                    mm.then_inc(pv_done, 1)

            def broadcast_inverse(g, quad):
                pe.wait_ge(inv_widened, QUADS * g + quad + 1)
                for t in range(QT):
                    mm = nc.tensor.matmul(attn[:, 1, t * P:(t + 1) * P],
                                          inv_wide[quad][:, t, :, :].rearrange("p h d -> p (h d)"),
                                          ident[:], start=True, stop=True)
                mm.then_inc(bcast_ready, 1)

            def output_projection(g):
                pe.wait_ge(attn_ready, QUADS * g + QUADS)
                bank = ring[USES.index(("out", 0)) % RING]
                for t in range(QT):
                    for quad in range(QUADS):
                        mm = nc.tensor.matmul(bank[:, t * D:(t + 1) * D], attn_T[quad][:, t * P:(t + 1) * P],
                                              wo[:, quad, :], start=(quad == 0), stop=(quad == QUADS - 1))
                mm.then_inc(out_proj_ready, 1)

            for j in range(AHEAD):
                scores(0, j, True)

            def attend(g, has_prev, has_cur, has_next):
                first = not has_prev
                for j in range(UNITS):
                    if has_cur:
                        if j + AHEAD < UNITS:
                            scores(g, j + AHEAD, first)
                        elif has_next:
                            scores(g + 1, j + AHEAD - UNITS, False)
                        pe.wait_ge(probs_ready, UNITS * g + j + 1)
                        transposes(g, j, 0, first)
                    s = j % 8
                    if s in PV_STEPS:
                        if j < 8 and has_prev:
                            values(g - 1, 1, PV_STEPS[s], False)
                        if j >= 8 and has_cur:
                            values(g, 0, PV_STEPS[s], first)
                    if s == R_STEP:
                        if j < 8 and has_prev:
                            broadcast_inverse(g - 1, 1)
                        if j >= 8 and has_cur:
                            broadcast_inverse(g, 0)
                    if has_cur:
                        transposes(g, j, 1, first)
                    if j == OUT_STEP - 1 and has_prev:
                        if has_cur:
                            ring_free(g, ("out", 0), first)
                        output_projection(g - 1)

            over_pairs(pe, attend)

        @block.scalar
        def _(act):
            nc.scalar.preload_act_table_set("natural_log_exp_and_others")
            for i in range(3):
                if i == 0:
                    act.wait_ge(weights_in, 16 * 3)
                nc.scalar.activation(w_hi[i][:], w_raw[i][:], ACT.Copy,
                                     scale=SCALE if i == 1 else 1.0).then_inc(w_hi_ready, 1)

            def split_x(b, h):
                n = HALVES * b + h
                act.wait_ge(xT_loaded[h], 16 * (b + 1))
                nc.scalar.activation(x_hi[h][:], xT_in[h][:], ACT.Copy).then_inc(x_hi_ready, 1)

            split_x(0, 0)
            act.wait_ge(consts_in, 16 * 7)
            act.wait_ge(bias_scaled, 1)

            def project(b, first, last):
                for h in range(HALVES):
                    n = HALVES * b + h
                    if h == 0 or not last:
                        if not (first and h == 0):
                            act.wait_ge(proj_ready, OUTS * n)
                        split_x(b + h, 1 - h)
                    if not first:
                        act.wait_ge(stored[h], 16 * 5 * b)
                    for i, (dst, bias) in enumerate(((k_out, bk_col), (k_out, bk_col), (q_out, bqs_col), (q_out, bqs_col))):
                        act.wait_ge(proj_ready, OUTS * n + i + 1)
                        m = i % DC
                        nc.scalar.activation(dst[h][:, m, 0, :], proj[:, i, :], ACT.Identity,
                                             bias=bias[:, m:m + 1]).then_inc(proj_hi_done, 1)

            over_steps(act, project)

            def log_adjacency(g, t):
                act.wait_ge(adj_clipped, QT * g + t + 1)
                nc.scalar.activation(log_adj[t][:], adj_in[t][:], ACT.Ln).then_inc(log_adj_ready, 1)

            def exponential(g, j):
                head, t = unit(j)
                act.wait_ge(logits_ready, UNITS * g + j + 1)
                nc.scalar.activation(probs[j % 2][:], neg_logits[j % LSLOTS][:], ACT.Exp,
                                     bias=neg_max[j % LSLOTS][:], scale=-1.0,
                                     accum_out=row_sum[j // 8][:, t, head % QH:head % QH + 1]
                                     ).then_inc(probs_ready, 1)

            for t in range(QT):
                log_adjacency(0, t)
            exponential(0, 0)
            for h in range(HALVES):
                act.wait_ge(stored[h], 16 * 5 * B)

            def copy_inverse(g, quad):
                act.wait_ge(bcast_ready, QUADS * g + quad + 1)
                nc.scalar.copy(inv_bcast[:], attn[:, 1, :]).then_inc(bcast_copied, 1)

            def attend(g, has_prev, has_cur, has_next):
                for j in range(UNITS):
                    if j == 0 and has_prev:
                        copy_inverse(g - 1, 0)
                    if j == 8 and has_prev:
                        copy_inverse(g - 1, 1)
                    if has_next and j == 12:
                        act.wait_ge(logits_ready, UNITS * g + 14)
                        log_adjacency(g + 1, 0)
                    if has_next and j == 14:
                        act.wait_ge(logits_ready, UNITS * g + 16)
                        log_adjacency(g + 1, 1)
                    if has_cur:
                        if j + 1 < UNITS:
                            exponential(g, j + 1)
                        elif has_next:
                            exponential(g + 1, 0)
                        head, t = unit(j)
                        if j % 8 == 0 and has_prev:
                            act.wait_ge(pv_done, QUADS * g + j // 8 - 1)
                        for half in range(2):
                            use = ("ab"[half], j)
                            if evacuator(use) == "scalar":
                                act.wait_ge(half_b_ready if half else half_a_ready, UNITS * g + j + 1)
                                nc.scalar.copy(probs_T[j // 8][:, head % QH, half * HK:(half + 1) * HK, t * P:(t + 1) * P],
                                               ring[USES.index(use) % RING][:, :].rearrange("p (k q) -> p k q", k=HK)
                                               ).then_inc(scalar_evac, 1)

            over_pairs(act, attend)

        @block.vector
        def _(dve):
            for i in range(3):
                dve.wait_ge(w_hi_ready, i + 1)
                nc.vector.scalar_tensor_tensor(w_lo[i][:], w_raw[i][:], SCALE if i == 1 else 1.0,
                                               w_hi[i][:].bitcast(F32), ALU.mult, ALU.subtract).then_inc(w_lo_ready, 1)

            def split_x(b, h):
                n = HALVES * b + h
                dve.wait_ge(x_hi_ready, n + 1)
                nc.vector.tensor_tensor(x_lo[h][:], xT_in[h][:], x_hi[h][:].bitcast(F32),
                                        ALU.subtract).then_inc(x_lo_ready, 1)

            split_x(0, 0)
            dve.wait_ge(consts_in, 16 * 7)
            nc.vector.tensor_scalar(bqs_col[:], bq_col[:], SCALE, None, ALU.mult).then_inc(bias_scaled, 1)
            dve.wait_ge(bias_scaled, 1)

            def project(b, first, last):
                for h in range(HALVES):
                    n = HALVES * b + h
                    if h == 0 or not last:
                        if not (first and h == 0):
                            dve.wait_ge(proj_ready, OUTS * n)
                        split_x(b + h, 1 - h)
                    if not first:
                        dve.wait_ge(stored[h], 16 * 5 * b)
                    for i, (dst, bias) in enumerate(((k_out, bk_col), (k_out, bk_col), (q_out, bqs_col), (q_out, bqs_col))):
                        dve.wait_ge(proj_hi_done, 4 * n + i + 1)
                        m = i % DC
                        nc.vector.scalar_tensor_tensor(dst[h][:, m, 1, :], proj[:, i, :], bias[:, m:m + 1],
                                                       dst[h][:, m, 0, :].bitcast(F32), ALU.add,
                                                       ALU.subtract).then_inc(proj_done, 1)
                    for i in (4, 5):
                        dve.wait_ge(proj_ready, OUTS * n + i + 1)
                        t = 2 * (i - 4)
                        nc.vector.tensor_tensor(v_out[h][:, t:t + 2, :],
                                                proj[:, i, :].rearrange("p (s d) -> p s d", s=2),
                                                bv_row[:].unsqueeze(1).broadcast_to([P, 2, D]),
                                                ALU.add).then_inc(proj_done, 1)

            over_steps(dve, project)

            def logits(g, j):
                head, t = unit(j)
                if j in (0, 2):
                    dve.wait_ge(log_adj_ready, QT * g + t + 1)
                count = at(dve, UNITS * g + j + 1)
                dve.wait_ge(bias_scaled, 1)
                dve.wait_ge(scores_ready, count)
                nc.vector.tensor_tensor_reduce(neg_logits[j % LSLOTS][:], score[j % 2][:], log_adj[t][:], -1.0,
                                               NEVER, ALU.add, ALU.min,
                                               neg_max[j % LSLOTS][:]).then_inc(logits_ready, 1)

            for j in range(AHEAD):
                logits(0, j)
            for h in range(HALVES):
                dve.wait_ge(stored[h], 16 * 5 * B)

            def inverse(g, quad):
                dve.wait_ge(probs_ready, UNITS * g + 8 * quad + 8)
                nc.vector.reciprocal(inv_sum[quad][:], row_sum[quad][:]).then_inc(inv_ready, 1)

            def normalise(g, quad):
                dve.wait_ge(bcast_copied, QUADS * g + quad + 1)
                nc.vector.tensor_tensor(attn_T[quad][:], attn[:, 0, :], inv_bcast[:], ALU.mult).then_inc(attn_ready, 1)

            def residual(g, first):
                dve.wait_ge(out_proj_ready, g + 1)
                dve.wait_ge(x_bo_ready, g + 1)
                if not first:
                    dve.wait_ge(normed_ready, g)
                nc.vector.tensor_tensor(resid[:], ring[USES.index(("out", 0)) % RING][:, :]
                                        .rearrange("p (s d) -> p s d", s=QT), x_bo[:], ALU.add).then_inc(resid_ready, 1)
                dve.wait_ge(resid_ready, g + 1)
                for t in range(QT):
                    nc.vector.bn_stats(stats[:, t, :], resid[:, t, :]).then_inc(bn_step, 1)
                count = at(dve, QT * g + QT)
                dve.wait_ge(bias_scaled, 1)
                dve.wait_ge(bn_step, count)
                for t in range(QT):
                    nc.vector.bn_aggr(mean_var[:, t, :], stats[:, t, :]).then_inc(stats_ready, 1)

            def attend(g, has_prev, has_cur, has_next):
                for j in range(UNITS):
                    if has_cur:
                        if j + AHEAD < UNITS:
                            logits(g, j + AHEAD)
                        elif has_next:
                            logits(g + 1, j + AHEAD - UNITS)
                    if j == 0 and has_prev:
                        normalise(g - 1, 0)
                    if j == 8 and has_prev:
                        normalise(g - 1, 1)
                    if j == 1 and has_prev:
                        inverse(g - 1, 1)
                    if j == 9 and has_cur:
                        inverse(g, 0)
                    if j == OUT_STEP and has_prev:
                        residual(g - 1, isinstance(g, int) and g == 1)
                    if has_cur:
                        head, t = unit(j)
                        if j % 8 == 0 and has_prev:
                            dve.wait_ge(pv_done, QUADS * g + j // 8 - 1)
                        for half in range(2):
                            use = ("ab"[half], j)
                            if evacuator(use) == "vector":
                                dve.wait_ge(half_b_ready if half else half_a_ready, UNITS * g + j + 1)
                                nc.vector.tensor_copy(probs_T[j // 8][:, head % QH, half * HK:(half + 1) * HK, t * P:(t + 1) * P],
                                                      ring[USES.index(use) % RING][:, :].rearrange("p (k q) -> p k q", k=HK)
                                                      ).then_inc(vector_evac, 1)

            over_pairs(dve, attend)

        @block.gpsimd
        def _(pool):
            nc.gpsimd.memset(ident[:], 0.0).then_inc(ln_step, 1)
            pool.wait_ge(ln_step, 1)
            nc.gpsimd.affine_select(out=ident[:], in_=ident[:], compare_op=ALU.not_equal, fill=1.0, base=0,
                                    pattern=[[-1, P]], channel_multiplier=1).then_inc(ident_ready, 1)
            nc.gpsimd.memset(minus_half[:], -0.5).then_inc(ln_step, 1)
            pool.wait_ge(ln_step, 2)
            pool.wait_ge(consts_in, 16 * 7)

            def clip(g):
                for t in range(QT):
                    count = at(pool, 16 * (g + 1))
                    pool.wait_ge(consts_in, 16 * 7)
                    pool.wait_ge(adj_loaded[t], count)
                    nc.gpsimd.tensor_scalar(adj_in[t][:], adj_in[t][:], ADJ_MIN, None, ALU.max).then_inc(adj_clipped, 1)

            clip(0)

            def layer_norm(g, first):
                steps = 4
                base = 2 + steps * g
                count = at(pool, QT * g + QT)
                pool.wait_ge(consts_in, 16 * 7)
                pool.wait_ge(stats_ready, count)
                nc.gpsimd.tensor_scalar(rstd[:, 0, :], mean_var[:, :, 1], LN_EPS, None, ALU.add).then_inc(ln_step, 1)
                pool.wait_ge(ln_step, base + 1)
                nc.gpsimd.tensor_tensor(rstd[:, 1, :], rstd[:, 0, :], minus_half[:], ALU.pow).then_inc(ln_step, 1)
                if not first:
                    pool.wait_ge(out_stored, 16 * g)
                count = at(pool, base + 2)
                pool.wait_ge(consts_in, 16 * 7)
                pool.wait_ge(ln_step, count)
                for t in range(QT):
                    ins = nc.gpsimd.tensor_scalar(normed[:, t, :], resid[:, t, :], mean_var[:, t, 0:1], rstd[:, 1, t:t + 1],
                                                  ALU.subtract, ALU.mult)
                ins.then_inc(ln_step, 1)
                pool.wait_ge(ln_step, base + 3)
                nc.gpsimd.tensor_tensor(normed[:], normed[:], gamma_row[:].unsqueeze(1).broadcast_to([P, QT, D]),
                                        ALU.mult).then_inc(ln_step, 1)
                pool.wait_ge(ln_step, base + 4)
                nc.gpsimd.tensor_tensor(normed[:], normed[:], beta_row[:].unsqueeze(1).broadcast_to([P, QT, D]),
                                        ALU.add).then_inc(normed_ready, 1)

            def widen(g, quad):
                count = at(pool, QUADS * g + quad + 1)
                pool.wait_ge(consts_in, 16 * 7)
                pool.wait_ge(inv_ready, count)
                nc.gpsimd.tensor_copy(inv_wide[quad][:], inv_sum[quad][:].unsqueeze(3)
                                      .broadcast_to([P, QT, QH, DK])).then_inc(inv_widened, 1)

            def attend(g, has_prev, has_cur, has_next):
                if has_prev:
                    widen(g - 1, 1)
                if has_next:
                    clip(g + 1)
                if has_cur:
                    widen(g, 0)
                if has_prev:
                    layer_norm(g - 1, isinstance(g, int) and g == 1)
                if has_cur:
                    pool.wait_ge(x_loaded, 16 * (g + 1))
                    nc.gpsimd.tensor_tensor(x_bo[:], x_bo[:], bo_row[:].unsqueeze(1).broadcast_to([P, QT, D]),
                                            ALU.add).then_inc(x_bo_ready, 1)

            over_pairs(pool, attend)


def kernel(x, adj, L0_gnn_Wq, L0_gnn_bq, L0_gnn_Wk, L0_gnn_bk, L0_gnn_Wv, L0_gnn_bv, L0_gnn_Wo, L0_gnn_bo,
           L0_gnn_gamma, L0_gnn_beta):
    import numpy as np
    import concourse.bacc as bacc
    from concourse.bass_utils import run_bass_kernel_spmd

    nc = bacc.Bacc("TRN2", target_bir_lowering=False, num_devices=1)
    arrays = {
        "x": x, "xT": np.swapaxes(x, 1, 2), "adj": adj,
        "wqT": np.transpose(L0_gnn_Wq), "wkT": np.transpose(L0_gnn_Wk),
        "wvT": np.transpose(L0_gnn_Wv), "woT": np.transpose(L0_gnn_Wo),
        "bq": np.transpose(np.reshape(L0_gnn_bq, (DC, P))), "bk": np.transpose(np.reshape(L0_gnn_bk, (DC, P))), "bv": L0_gnn_bv, "bo": L0_gnn_bo,
        "gamma": L0_gnn_gamma, "beta": L0_gnn_beta,
    }
    arrays = {name: np.ascontiguousarray(a) for name, a in arrays.items()}
    args = {name: nc.dram_tensor(name, a.shape, mybir.dt.from_np(a.dtype), kind="ExternalInput").ap()
            for name, a in arrays.items()}
    out = nc.dram_tensor("out", x.shape, F32, kind="ExternalOutput").ap()
    graph_attention(nc, out=out, **args)
    r = run_bass_kernel_spmd(nc, [arrays], core_ids=[0])
    return r.results[0]["out"]
```

```python
from contextlib import ExitStack

import concourse.bass as bass
from concourse import mybir

F32 = mybir.dt.float32
F32R = mybir.dt.float32r
ALU = mybir.AluOpType
ACT = mybir.ActivationFunctionType

P = 128
B, N, D, H = 8, 1024, 256, 8
DK = D // H
DC = D // P
SCALE = float(DK) ** -0.5
LN_EPS = 1e-05
ADJ_MIN = 1e-08
NEVER = 3.0e38

HALVES = 2
TOK = N // HALVES
TT = TOK // P
OUTS = 6

QT = 2
PAIR = QT * P
PAIRS = B * N // PAIR
PPB = N // PAIR
UNITS = H * QT
QUADS = 2
QH = H // QUADS
KT = N // P
HK = KT // 2
AHEAD = 3
EXP_AHEAD = 2
LSLOTS = 4
PSLOTS = 4
LOG_STEPS = (11, 14)
GROUPS = P // DK

K_PART = [0, 1, 0, 1]
Q_PART = [0, 0, 1, 1]

HALF = UNITS // QUADS
PV_STEPS = {1: (0,), 2: (1,), 3: (2,), 4: (3, 4), 5: (5,), 6: (6,), 7: (7,)}
INV_STEP = 5
OUT_STEP = 10

RING = 3
USES = []
for _j in range(UNITS):
    USES.append(("a", _j))
    if _j % HALF == INV_STEP:
        USES.append(("inv", 1 - _j // HALF))
    if _j - OUT_STEP in range(QT):
        USES.append(("out", _j - OUT_STEP))
    USES.append(("b", _j))
STATS_STEPS = (13, 14)
assert len(USES) % RING == 0 and (USES.index(("out", 1)) - USES.index(("out", 0))) == RING
SCALAR_TAKES_A = (1, 8)


def unit(j):
    return 2 * (j // 4) + j % 2, (j % 4) // 2


def evacuator(use):
    return "vector" if use[0] == "a" and use[1] not in SCALAR_TAKES_A else "scalar"


def evacuated(use, engine):
    return sum(x[0] in "ab" and evacuator(x) == engine for x in USES[:USES.index(use) + 1])


VECTOR_EVACS = evacuated(USES[-1], "vector")
SCALAR_EVACS = evacuated(USES[-1], "scalar")


def bank_of(use):
    return USES.index(use) % RING


def graph_attention(nc, x, xT, adj, wqT, wkT, wvT, woT, bq, bk, bv, bo, gamma, beta, out):
    x_rows = x.rearrange("b t d -> (b t) d")
    adj_rows = adj.rearrange("b q k -> (b q) k")
    out_rows = out.rearrange("b t d -> (b t) d")
    q_dram = nc.dram_tensor("q_parts", (2 * D, B * N), F32, kind="Internal").ap()
    k_dram = nc.dram_tensor("k_parts", (2 * D, B * N), F32, kind="Internal").ap()
    v_dram = nc.dram_tensor("v_scratch", (B * N, D), F32, kind="Internal").ap()
    q_store = q_dram.rearrange("(l m p) t -> p m l t", l=2, m=DC)
    k_store = k_dram.rearrange("(l m p) t -> p m l t", l=2, m=DC)

    with ExitStack() as ctx:
        def sb(name, shape, dt=F32, scope=ctx):
            return scope.enter_context(nc.sbuf_tensor(name, shape, dt))

        def sem(name):
            return ctx.enter_context(nc.semaphore(name))

        ident = sb("ident", [P, P])
        bq_col = sb("bq_col", [P, DC])
        bqs_col = sb("bqs_col", [P, DC])
        bk_col = sb("bk_col", [P, DC])
        bv_row = sb("bv_row", [P, D])
        bo_row = sb("bo_row", [P, D])
        gamma_row = sb("gamma_row", [P, D])
        beta_row = sb("beta_row", [P, D])
        wo = sb("wo", [P, DC, D])
        minus_half = sb("minus_half", [P, QT])
        k_stack = sb("k_stack", [P, H, N], F32R)
        q_stack = [sb(f"q_stack{q}", [P, QH, PAIR], F32R) for q in range(QUADS)]
        v_sb = [sb(f"v_sb{q}", [P, KT, P]) for q in range(QUADS)]
        adj_in = [sb(f"adj_in{t}", [P, N]) for t in range(QT)]
        log_adj = [sb(f"log_adj{t}", [P, N]) for t in range(QT)]
        neg_logits = [sb(f"neg_logits{s}", [P, N]) for s in range(LSLOTS)]
        neg_max = [sb(f"neg_max{s}", [P, 1]) for s in range(LSLOTS)]
        probs = [sb(f"probs{s}", [P, N]) for s in range(PSLOTS)]
        row_sum = [sb(f"row_sum{q}", [P, QT, QH]) for q in range(QUADS)]
        inv_sum = [sb(f"inv_sum{q}", [P, QT, QH]) for q in range(QUADS)]
        inv_wide = [sb(f"inv_wide{q}", [P, QT, QH, DK]) for q in range(QUADS)]
        inv_bcast = [sb(f"inv_bcast{q}", [P, PAIR]) for q in range(QUADS)]
        attn_T = [sb(f"attn_T{q}", [P, PAIR]) for q in range(QUADS)]
        x_bo = sb("x_bo", [P, QT, D])
        resid = sb("resid", [P, QT, D])
        stats = sb("stats", [P, QT, 6])
        mean_var = sb("mean_var", [P, QT, 2])
        rstd = sb("rstd", [P, 2, QT])
        normed = sb("normed", [P, QT, D])

        with ExitStack() as early:
            w_raw = [sb(f"w_raw{i}", [P, DC, D], F32, early) for i in range(3)]
            w_hi = [sb(f"w_hi{i}", [P, DC, D], F32R, early) for i in range(3)]
            w_lo = [sb(f"w_lo{i}", [P, DC, D], F32R, early) for i in range(3)]
            xT_in = [sb(f"xT_in{h}", [P, DC, TOK], F32, early) for h in range(HALVES)]
            x_hi = [sb(f"x_hi{h}", [P, DC, TOK], F32R, early) for h in range(HALVES)]
            x_lo = [sb(f"x_lo{h}", [P, DC, TOK], F32R, early) for h in range(HALVES)]
            k_out, q_out, v_out = [], [], []
            for h in range(HALVES):
                if h == 1:
                    used = 4 * ((9 * DC * D + 6 * DC * TOK) + (2 * DC * 2 * TOK + TT * D))
                    sb("gap", [P, (QUADS * QH * KT * PAIR * 4 - used) // 4], F32, early)
                k_out.append(sb(f"k_out{h}", [P, DC, 2, TOK], F32R, early))
                q_out.append(sb(f"q_out{h}", [P, DC, 2, TOK], F32R, early))
                v_out.append(sb(f"v_out{h}", [P, TT, D], F32, early))
        probs_T = [sb(f"probs_T{q}", [P, QH, KT, PAIR]) for q in range(QUADS)]

        with nc.psum_tensor("proj", [P, OUTS, TOK], F32) as proj:
            pass
        score = [ctx.enter_context(nc.psum_tensor(f"score{s}", [P, N], F32)) for s in range(2)]
        ring = [ctx.enter_context(nc.psum_tensor(f"ring{s}", [P, TOK], F32)) for s in range(RING)]
        attn = ctx.enter_context(nc.psum_tensor("attn", [P, TOK], F32))

        weights_in = [sem(f"weights_in_{n}") for n in "kqv"]
        biases_in = sem("biases_in")
        consts_in = sem("consts_in")
        ident_ready = sem("ident_ready")
        bias_scaled = sem("bias_scaled")
        w_hi_ready = sem("w_hi_ready")
        w_lo_ready = sem("w_lo_ready")
        xT_loaded = [sem(f"xT_loaded{h}") for h in range(HALVES)]
        x_hi_ready = sem("x_hi_ready")
        x_lo_ready = sem("x_lo_ready")
        proj_ready = sem("proj_ready")
        proj_hi_done = sem("proj_hi_done")
        proj_done = sem("proj_done")
        stored = [sem(f"stored{h}") for h in range(HALVES)]

        k_loaded = [sem(f"k_loaded{i}") for i in range(H // 2)]
        q_loaded = [sem(f"q_loaded{q}") for q in range(QUADS)]
        v_loaded = [sem(f"v_loaded{q}") for q in range(QUADS)]
        adj_loaded = [sem(f"adj_loaded{t}") for t in range(QT)]
        x_loaded = sem("x_loaded")
        adj_clipped = sem("adj_clipped")
        log_adj_ready = sem("log_adj_ready")
        scores_ready = sem("scores_ready")
        logits_ready = sem("logits_ready")
        probs_ready = sem("probs_ready")
        half_a_ready = sem("half_a_ready")
        half_b_ready = sem("half_b_ready")
        vector_evac = sem("vector_evac")
        scalar_evac = sem("scalar_evac")
        inv_ready = sem("inv_ready")
        inv_widened = sem("inv_widened")
        pv_done = sem("pv_done")
        inv_broadcast = sem("inv_broadcast")
        inv_copied = sem("inv_copied")
        attn_ready = sem("attn_ready")
        out_proj_ready = sem("out_proj_ready")
        x_bo_ready = sem("x_bo_ready")
        resid_ready = sem("resid_ready")
        bn_step = sem("bn_step")
        stats_ready = sem("stats_ready")
        ln_step = sem("ln_step")
        normed_ready = sem("normed_ready")
        out_stored = sem("out_stored")

        def over_steps(eng, body):
            body(0, True, False)
            with eng.Fori(1, B - 1) as b:
                body(b, False, False)
            body(B - 1, False, True)

        def over_pairs(eng, body):
            body(0, False, True, True)
            with eng.Fori(1, PAIRS - 1) as g:
                body(g, True, True, True)
            body(PAIRS - 1, True, True, False)
            body(PAIRS, True, False, False)

        def at(eng, value):
            return value if isinstance(value, int) else eng.to_reg(value)

        block = ctx.enter_context(nc.Block())

        @block.sync
        def _(sp):
            def load_weights(i, w):
                sp.dma_start(w_raw[i][:], w.rearrange("(c p) n -> p c n", p=P)).then_inc(weights_in[i], 16)

            def load_xT(b, h):
                sp.dma_start(xT_in[h][:], xT.rearrange("b (c p) t -> p b c t", p=P)
                             [:, bass.ds(b, 1), :, h * TOK:(h + 1) * TOK].rearrange("p o c t -> p (o c) t")).then_inc(xT_loaded[h], 16)

            load_weights(0, wkT)
            load_xT(0, 0)
            load_weights(1, wqT)
            sp.dma_start(bk_col[:], bk).then_inc(biases_in, 16)
            sp.dma_start(bq_col[:], bq).then_inc(biases_in, 16)
            load_weights(2, wvT)
            sp.dma_start(bv_row[:], bv.partition_broadcast(P)).then_inc(biases_in, 16)
            load_xT(0, 1)
            for row, vec in ((bo_row, bo), (gamma_row, gamma), (beta_row, beta)):
                sp.dma_start(row[:], vec.partition_broadcast(P)).then_inc(consts_in, 16)
            sp.dma_start(wo[:], woT.rearrange("(c p) n -> p c n", p=P)).then_inc(consts_in, 16)

            def load_k(i, b):
                for gr in range(GROUPS):
                    row = K_PART[gr] * D + 2 * i * DK
                    sp.dma_start(k_stack[gr * DK:(gr + 1) * DK, 2 * i:2 * i + 2, :].bitcast(F32),
                                 k_dram[row:row + 2 * DK, bass.ds(b * N, N)]
                                 .rearrange("(h d) t -> d h t", h=2)).then_inc(k_loaded[i], 16)

            def load_q(q, g):
                for gr in range(GROUPS):
                    row = Q_PART[gr] * D + q * P
                    sp.dma_start(q_stack[q][gr * DK:(gr + 1) * DK, :, :].bitcast(F32),
                                 q_dram[row:row + P, bass.ds(g * PAIR, PAIR)]
                                 .rearrange("(h d) t -> d h t", h=QH)).then_inc(q_loaded[q], 16)

            def load_v(q, b):
                sp.dma_start(v_sb[q][:], v_dram[bass.ds(b * N, N), q * P:(q + 1) * P]
                             .rearrange("(k p) d -> p k d", p=P)).then_inc(v_loaded[q], 16)

            def load_adj(t, g):
                sp.dma_start(adj_in[t][:], adj_rows[bass.ds(g * PAIR + t * P, P), :]).then_inc(adj_loaded[t], 16)

            def project(b, first, last):
                for h in range(HALVES):
                    n = HALVES * b + h
                    if not last:
                        sp.wait_ge(weights_in[0], 16)
                        sp.wait_ge(x_hi_ready, n + 1)
                        sp.wait_ge(x_lo_ready, n + 1)
                        load_xT(b + 1, h)
                    elif h == 0:
                        load_adj(0, 0)
                        for half in range(HALVES):
                            sp.wait_ge(stored[half], 16 * 5)
                        load_k(0, 0)
                        load_q(0, 0)
                        load_adj(1, 0)
                        load_k(1, 0)
                        load_k(2, 0)
                        load_q(1, 0)
                        load_v(0, 0)
                    else:
                        load_k(3, 0)
                        load_v(1, 0)
                        for t in range(QT):
                            sp.wait_ge(log_adj_ready, t + 1)
                            load_adj(t, 1)
                    for dst, src, done in ((k_store, k_out[h], 2), (q_store, q_out[h], 4)):
                        count = at(sp, OUTS * n + done)
                        sp.wait_ge(weights_in[0], 16)
                        sp.wait_ge(proj_done, count)
                        for m in range(DC):
                            sp.dma_start(dst[:, m, :, bass.ds(n * TOK, TOK)],
                                         src[:, m].bitcast(F32)).then_inc(stored[h], 16)
                    count = at(sp, OUTS * n + OUTS)
                    sp.wait_ge(weights_in[0], 16)
                    sp.wait_ge(proj_done, count)
                    sp.dma_start(v_dram[bass.ds(n * TOK, TOK), :].rearrange("(k p) d -> p k d", p=P),
                                 v_out[h][:]).then_inc(stored[h], 16)

            over_steps(sp, project)

            def attend(g, batch, new_batch, last_of_batch, more, more_adj):
                if new_batch:
                    count = at(sp, QUADS * g - 1)
                    sp.wait_ge(weights_in[0], 16)
                    sp.wait_ge(pv_done, count)
                    load_v(0, batch)
                if last_of_batch and more:
                    count = at(sp, UNITS * g + 4)
                    sp.wait_ge(weights_in[0], 16)
                    sp.wait_ge(scores_ready, count)
                    load_k(0, batch + 1)
                if more:
                    count = at(sp, UNITS * g + 8)
                    sp.wait_ge(weights_in[0], 16)
                    sp.wait_ge(scores_ready, count)
                    load_q(0, g + 1)
                    if last_of_batch:
                        load_k(1, batch + 1)
                if new_batch:
                    count = at(sp, QUADS * g)
                    sp.wait_ge(weights_in[0], 16)
                    sp.wait_ge(pv_done, count)
                    load_v(1, batch)
                if last_of_batch and more:
                    count = at(sp, UNITS * g + 12)
                    sp.wait_ge(weights_in[0], 16)
                    sp.wait_ge(scores_ready, count)
                    load_k(2, batch + 1)
                if not (isinstance(g, int) and g == 0):
                    count = at(sp, QT * g)
                    sp.wait_ge(weights_in[0], 16)
                    sp.wait_ge(resid_ready, count)
                sp.dma_start(x_bo[:], x_rows[bass.ds(g * PAIR, PAIR), :]
                             .rearrange("(s p) d -> p s d", p=P)).then_inc(x_loaded, 16)
                if more:
                    count = at(sp, UNITS * g + 16)
                    sp.wait_ge(weights_in[0], 16)
                    sp.wait_ge(scores_ready, count)
                    load_q(1, g + 1)
                    if last_of_batch:
                        load_k(3, batch + 1)
                if more_adj:
                    for t in range(QT):
                        count = at(sp, QT * g + QT + t + 1)
                        sp.wait_ge(weights_in[0], 16)
                        sp.wait_ge(log_adj_ready, count)
                        load_adj(t, g + 2)
                if not (isinstance(g, int) and g == 0):
                    store_out(g - 1)

            def store_out(g):
                count = at(sp, g + 1)
                sp.wait_ge(weights_in[0], 16)
                sp.wait_ge(normed_ready, count)
                sp.dma_start(out_rows[bass.ds(g * PAIR, PAIR), :].rearrange("(s p) d -> p s d", p=P),
                             normed[:]).then_inc(out_stored, 16)

            def batch_of_pairs(b, first, last):
                g = PPB * b
                attend(g, b, not first, False, True, True)
                attend(g + 1, b, False, False, True, True)
                attend(g + 2, b, False, False, True, not last)
                if first:
                    for h in range(HALVES):
                        sp.wait_ge(stored[h], 16 * 5 * B)
                attend(g + 3, b, False, True, not last, not last)

            over_steps(sp, batch_of_pairs)
            store_out(PAIRS - 1)
            sp.wait_ge(out_stored, 16 * PAIRS)

        @block.tensor
        def _(pe):

            def project(b, first, last):
                for h in range(HALVES):
                    n = HALVES * b + h
                    pe.wait_ge(x_hi_ready, n + 1)
                    pe.wait_ge(x_lo_ready, n + 1)
                    for i, w in ((0, 0), (1, 0), (2, 1), (3, 1)):
                        if not (first and h == 0):
                            pe.wait_ge(proj_done, OUTS * (n - 1) + i + 1)
                        if first and h == 0:
                            pe.wait_ge(w_hi_ready, w + 1)
                            pe.wait_ge(w_lo_ready, w + 1)
                        m = i % DC
                        terms = [(wp, xp, c) for c in range(DC)
                                 for wp, xp in ((w_hi, x_hi), (w_hi, x_lo), (w_lo, x_hi))]
                        for s, (wp, xp, c) in enumerate(terms):
                            mm = nc.tensor.matmul(proj[:, i, :], wp[w][:, c, m * P:(m + 1) * P], xp[h][:, c, :],
                                                  start=(s == 0), stop=(s == len(terms) - 1))
                        mm.then_inc(proj_ready, 1)
                    if first and h == 0:
                        pe.wait_ge(w_hi_ready, 3)
                        pe.wait_ge(w_lo_ready, 3)
                    for i in (4, 5):
                        if not (first and h == 0):
                            pe.wait_ge(proj_done, OUTS * (n - 1) + i + 1)
                        for half in range(2):
                            t = 2 * (i - 4) + half
                            terms = [(xp, wp, c) for c in range(DC)
                                     for xp, wp in ((x_hi, w_hi), (x_lo, w_hi), (x_hi, w_lo))]
                            for s, (xp, wp, c) in enumerate(terms):
                                mm = nc.tensor.matmul(proj[:, i, half * D:(half + 1) * D],
                                                      xp[h][:, c, t * P:(t + 1) * P], wp[2][:, c, :],
                                                      start=(s == 0), stop=(s == len(terms) - 1))
                        mm.then_inc(proj_ready, 1)

            over_steps(pe, project)

            pe.wait_ge(proj_done, OUTS * HALVES * B)
            pe.wait_ge(ident_ready, 1)
            pe.wait_ge(consts_in, 16 * 4)

            def scores(g, j, first):
                head, t = unit(j)
                quad = j // HALF
                if j % HALF == 0:
                    pe.wait_ge(q_loaded[quad], 16 * GROUPS * (g + 1))
                if j % 4 == 0:
                    pe.wait_ge(k_loaded[j // 4], 16 * GROUPS * ((g >> 2) + 1))
                if not (first and j < 2):
                    pe.wait_ge(logits_ready, UNITS * g + j - 1)
                for n in range(2):
                    mm = nc.tensor.matmul(score[j % 2][:, n * TOK:(n + 1) * TOK],
                                          q_stack[quad][:, head % QH, t * P:(t + 1) * P],
                                          k_stack[:, head, n * TOK:(n + 1) * TOK], start=True, stop=True)
                mm.then_inc(scores_ready, 1)

            def ring_free(g, use, first):
                i = USES.index(use)
                before = USES[(i - RING) % len(USES)]
                pairs_back = 1 if i < RING else 0
                if first and (pairs_back or before[0] == "out" or before == ("inv", 1)):
                    return
                if before[0] == "out":
                    pe.wait_ge(resid_ready, QT * (g - 1) + before[1] + 1)
                elif before[0] == "inv":
                    pe.wait_ge(inv_copied, QUADS * g + 1 - before[1])
                elif evacuator(before) == "vector":
                    pe.wait_ge(vector_evac, VECTOR_EVACS * (g - pairs_back) + evacuated(before, "vector"))
                else:
                    pe.wait_ge(scalar_evac, SCALAR_EVACS * (g - pairs_back) + evacuated(before, "scalar"))

            def transposes(g, j, half, first):
                use = ("ab"[half], j)
                ring_free(g, use, first)
                bank = ring[bank_of(use)]
                for k in range(HK):
                    kt = half * HK + k
                    mm = nc.tensor.transpose(bank[:, k * P:(k + 1) * P],
                                             probs[j % PSLOTS][:, kt * P:(kt + 1) * P], ident[:])
                mm.then_inc(half_b_ready if half else half_a_ready, 1)

            def values(g, quad, kt, first):
                if kt in (0, HK):
                    last = ("b" if kt else "a", HALF * quad + HALF - 1)
                    pe.wait_ge(vector_evac, VECTOR_EVACS * g + evacuated(last, "vector"))
                    pe.wait_ge(scalar_evac, SCALAR_EVACS * g + evacuated(last, "scalar"))
                if kt == 0:
                    pe.wait_ge(v_loaded[quad], 16 * ((g >> 2) + 1))
                    if not (first and quad == 0):
                        pe.wait_ge(attn_ready, QUADS * g + quad)
                for hh in range(QH):
                    mm = nc.tensor.matmul(attn[hh * DK:(hh + 1) * DK, 0:PAIR],
                                          v_sb[quad][:, kt, hh * DK:(hh + 1) * DK],
                                          probs_T[quad][:, hh, kt, :], start=(kt == 0), stop=(kt == KT - 1))
                if kt == KT - 1:
                    mm.then_inc(pv_done, 1)

            def broadcast_inverse(g, quad):
                pe.wait_ge(inv_widened, QUADS * g + quad + 1)
                for t in range(QT):
                    mm = nc.tensor.transpose(ring[bank_of(("inv", quad))][:, t * P:(t + 1) * P],
                                             inv_wide[quad][:, t, :, :].rearrange("p h d -> p (h d)"), ident[:])
                mm.then_inc(inv_broadcast, 1)

            def output_projection(g, t):
                if t == 0:
                    pe.wait_ge(attn_ready, QUADS * g + QUADS)
                for quad in range(QUADS):
                    mm = nc.tensor.matmul(ring[bank_of(("out", t))][:, 0:D], attn_T[quad][:, t * P:(t + 1) * P],
                                          wo[:, quad, :], start=(quad == 0), stop=(quad == QUADS - 1))
                mm.then_inc(out_proj_ready, 1)

            for j in range(AHEAD):
                scores(0, j, True)

            def attend(g, has_prev, has_cur, has_next):
                first = not has_prev
                if not has_cur:
                    pe.wait_ge(vector_evac, VECTOR_EVACS * g)
                    pe.wait_ge(scalar_evac, SCALAR_EVACS * g)
                for j in range(UNITS):
                    if has_cur:
                        if j + AHEAD < UNITS:
                            scores(g, j + AHEAD, first)
                        elif has_next:
                            scores(g + 1, j + AHEAD - UNITS, False)
                        pe.wait_ge(probs_ready, UNITS * g + j + 1)
                        transposes(g, j, 0, first)
                    for kt in PV_STEPS.get(j % HALF, ()):
                        if j < HALF and has_prev:
                            values(g - 1, 1, kt, False)
                        if j >= HALF and has_cur:
                            values(g, 0, kt, first)
                    if j == INV_STEP and has_prev:
                        if has_cur:
                            ring_free(g, ("inv", 1), False)
                        broadcast_inverse(g - 1, 1)
                    if j == HALF + INV_STEP and has_cur:
                        ring_free(g, ("inv", 0), first)
                        broadcast_inverse(g, 0)
                    if j - OUT_STEP in range(QT) and has_prev:
                        if has_cur or j > OUT_STEP:
                            ring_free(g, ("out", j - OUT_STEP), first)
                        output_projection(g - 1, j - OUT_STEP)
                    if has_cur:
                        transposes(g, j, 1, first)

            over_pairs(pe, attend)

        @block.scalar
        def _(act):
            nc.scalar.preload_act_table_set("natural_log_exp_and_others")

            def split_weights(i):
                act.wait_ge(weights_in[i], 16)
                nc.scalar.activation(w_hi[i][:], w_raw[i][:], ACT.Copy,
                                     scale=SCALE if i == 1 else 1.0).then_inc(w_hi_ready, 1)

            def split_x(b, h):
                n = HALVES * b + h
                act.wait_ge(xT_loaded[h], 16 * (b + 1))
                nc.scalar.activation(x_hi[h][:], xT_in[h][:], ACT.Copy).then_inc(x_hi_ready, 1)

            split_weights(0)
            split_x(0, 0)
            split_weights(1)
            split_weights(2)
            act.wait_ge(biases_in, 16 * 3)
            act.wait_ge(bias_scaled, 1)

            def project(b, first, last):
                for h in range(HALVES):
                    n = HALVES * b + h
                    if h == 0 or not last:
                        if not (first and h == 0):
                            act.wait_ge(proj_ready, OUTS * n)
                        split_x(b + h, 1 - h)
                    if not first:
                        act.wait_ge(stored[h], 16 * 5 * b)
                    for i, (dst, bias) in enumerate(((k_out, bk_col), (k_out, bk_col), (q_out, bqs_col), (q_out, bqs_col))):
                        act.wait_ge(proj_ready, OUTS * n + i + 1)
                        m = i % DC
                        nc.scalar.activation(dst[h][:, m, 0, :], proj[:, i, :], ACT.Identity,
                                             bias=bias[:, m:m + 1]).then_inc(proj_hi_done, 1)

            over_steps(act, project)

            def log_adjacency(g, t):
                act.wait_ge(adj_clipped, QT * g + t + 1)
                nc.scalar.activation(log_adj[t][:], adj_in[t][:], ACT.Ln).then_inc(log_adj_ready, 1)

            def exponential(g, j):
                head, t = unit(j)
                act.wait_ge(logits_ready, UNITS * g + j + 1)
                nc.scalar.activation(probs[j % PSLOTS][:], neg_logits[j % LSLOTS][:], ACT.Exp,
                                     bias=neg_max[j % LSLOTS][:], scale=-1.0,
                                     accum_out=row_sum[j // HALF][:, t, head % QH:head % QH + 1]
                                     ).then_inc(probs_ready, 1)

            for j in range(EXP_AHEAD):
                log_adjacency(0, j)
                exponential(0, j)

            def copy_inverse(g, quad):
                act.wait_ge(inv_broadcast, QUADS * g + quad + 1)
                nc.scalar.copy(inv_bcast[quad][:], ring[bank_of(("inv", quad))][:, 0:PAIR]).then_inc(inv_copied, 1)

            def attend(g, has_prev, has_cur, has_next):
                for j in range(UNITS):
                    if has_next and j in LOG_STEPS:
                        t = LOG_STEPS.index(j)
                        act.wait_ge(logits_ready, UNITS * g + 14 + 2 * t)
                        log_adjacency(g + 1, t)
                    if has_cur:
                        if j + EXP_AHEAD < UNITS:
                            exponential(g, j + EXP_AHEAD)
                        elif has_next:
                            exponential(g + 1, j + EXP_AHEAD - UNITS)
                        head, t = unit(j)
                        if j == HALF and not has_prev:
                            act.wait_ge(stored[0], 16 * 5 * B)
                        if j % HALF == 0 and has_prev:
                            act.wait_ge(pv_done, QUADS * g + j // HALF - 1)
                    if j == INV_STEP and has_prev:
                        copy_inverse(g - 1, 1)
                    if j == HALF + INV_STEP and has_cur:
                        copy_inverse(g, 0)
                    if has_cur:
                        for half in range(2):
                            use = ("ab"[half], j)
                            if evacuator(use) == "scalar":
                                act.wait_ge(half_b_ready if half else half_a_ready, UNITS * g + j + 1)
                                nc.scalar.copy(probs_T[j // HALF][:, head % QH, half * HK:(half + 1) * HK, t * P:(t + 1) * P],
                                               ring[bank_of(use)][:, :].rearrange("p (k q) -> p k q", k=HK)
                                               ).then_inc(scalar_evac, 1)

            over_pairs(act, attend)

        @block.vector
        def _(dve):
            def split_weights(i):
                dve.wait_ge(w_hi_ready, i + 1)
                nc.vector.scalar_tensor_tensor(w_lo[i][:], w_raw[i][:], SCALE if i == 1 else 1.0,
                                               w_hi[i][:].bitcast(F32), ALU.mult, ALU.subtract).then_inc(w_lo_ready, 1)

            def split_x(b, h):
                n = HALVES * b + h
                dve.wait_ge(x_hi_ready, n + 1)
                nc.vector.tensor_tensor(x_lo[h][:], xT_in[h][:], x_hi[h][:].bitcast(F32),
                                        ALU.subtract).then_inc(x_lo_ready, 1)

            split_weights(0)
            split_x(0, 0)
            split_weights(1)
            split_weights(2)
            dve.wait_ge(biases_in, 16 * 3)
            nc.vector.tensor_scalar(bqs_col[:], bq_col[:], SCALE, None, ALU.mult).then_inc(bias_scaled, 1)
            dve.wait_ge(bias_scaled, 1)

            def project(b, first, last):
                for h in range(HALVES):
                    n = HALVES * b + h
                    if h == 0 or not last:
                        if not (first and h == 0):
                            dve.wait_ge(proj_ready, OUTS * n)
                        split_x(b + h, 1 - h)
                    if not first:
                        dve.wait_ge(stored[h], 16 * 5 * b)
                    for i, (dst, bias) in enumerate(((k_out, bk_col), (k_out, bk_col), (q_out, bqs_col), (q_out, bqs_col))):
                        dve.wait_ge(proj_hi_done, 4 * n + i + 1)
                        m = i % DC
                        nc.vector.scalar_tensor_tensor(dst[h][:, m, 1, :], proj[:, i, :], bias[:, m:m + 1],
                                                       dst[h][:, m, 0, :].bitcast(F32), ALU.add,
                                                       ALU.subtract).then_inc(proj_done, 1)
                    for i in (4, 5):
                        dve.wait_ge(proj_ready, OUTS * n + i + 1)
                        t = 2 * (i - 4)
                        nc.vector.tensor_tensor(v_out[h][:, t:t + 2, :],
                                                proj[:, i, :].rearrange("p (s d) -> p s d", s=2),
                                                bv_row[:].unsqueeze(1).broadcast_to([P, 2, D]),
                                                ALU.add).then_inc(proj_done, 1)

            over_steps(dve, project)

            def logits(g, j):
                head, t = unit(j)
                if j in (0, 2):
                    dve.wait_ge(log_adj_ready, QT * g + t + 1)
                count = at(dve, UNITS * g + j + 1)
                dve.wait_ge(bias_scaled, 1)
                dve.wait_ge(scores_ready, count)
                nc.vector.tensor_tensor_reduce(neg_logits[j % LSLOTS][:], score[j % 2][:], log_adj[t][:], -1.0,
                                               NEVER, ALU.add, ALU.min,
                                               neg_max[j % LSLOTS][:]).then_inc(logits_ready, 1)

            for j in range(AHEAD):
                logits(0, j)

            def inverse(g, quad):
                dve.wait_ge(probs_ready, UNITS * g + 8 * quad + 8)
                nc.vector.reciprocal(inv_sum[quad][:], row_sum[quad][:]).then_inc(inv_ready, 1)

            def normalise(g, quad):
                dve.wait_ge(pv_done, QUADS * g + quad + 1)
                dve.wait_ge(inv_copied, QUADS * g + quad + 1)
                nc.vector.tensor_tensor(attn_T[quad][:], attn[:, 0:PAIR], inv_bcast[quad][:],
                                        ALU.mult).then_inc(attn_ready, 1)

            def residual(g, t, first):
                dve.wait_ge(out_proj_ready, QT * g + t + 1)
                if t == 0:
                    dve.wait_ge(x_bo_ready, g + 1)
                    if not first:
                        dve.wait_ge(normed_ready, g)
                nc.vector.tensor_tensor(resid[:, t, :], ring[bank_of(("out", t))][:, 0:D], x_bo[:, t, :],
                                        ALU.add).then_inc(resid_ready, 1)

            def statistics(g, t):
                dve.wait_ge(resid_ready, QT * g + t + 1)
                nc.vector.bn_stats(stats[:, t, :], resid[:, t, :]).then_inc(bn_step, 1)

            def mean_variance(g):
                count = at(dve, QT * g + QT)
                dve.wait_ge(bias_scaled, 1)
                dve.wait_ge(bn_step, count)
                for t in range(QT):
                    nc.vector.bn_aggr(mean_var[:, t, :], stats[:, t, :]).then_inc(stats_ready, 1)

            def attend(g, has_prev, has_cur, has_next):
                for j in range(UNITS):
                    if j % HALF == 0 and has_prev:
                        normalise(g - 1, j // HALF)
                    if has_cur:
                        if j + AHEAD < UNITS:
                            logits(g, j + AHEAD)
                        elif has_next:
                            logits(g + 1, j + AHEAD - UNITS)
                    if has_cur:
                        head, t = unit(j)
                        for half in range(2):
                            use = ("ab"[half], j)
                            if j == HALF and not has_prev and half == 0:
                                dve.wait_ge(stored[0], 16 * 5 * B)
                            if j % HALF == 0 and has_prev and half == 0:
                                dve.wait_ge(pv_done, QUADS * g + j // HALF - 1)
                            if evacuator(use) == "vector":
                                dve.wait_ge(half_b_ready if half else half_a_ready, UNITS * g + j + 1)
                                nc.vector.tensor_copy(probs_T[j // HALF][:, head % QH, half * HK:(half + 1) * HK, t * P:(t + 1) * P],
                                                      ring[bank_of(use)][:, :].rearrange("p (k q) -> p k q", k=HK)
                                                      ).then_inc(vector_evac, 1)
                    if j % HALF == HALF - 1 and has_cur:
                        inverse(g, j // HALF)
                    if j - OUT_STEP in range(QT) and has_prev:
                        residual(g - 1, j - OUT_STEP, isinstance(g, int) and g == 1)
                    if j in STATS_STEPS and has_prev:
                        statistics(g - 1, STATS_STEPS.index(j))
                    if j == UNITS - 1 and has_prev:
                        mean_variance(g - 1)

            over_pairs(dve, attend)

        @block.gpsimd
        def _(pool):
            nc.gpsimd.memset(ident[:], 0.0).then_inc(ln_step, 1)
            pool.wait_ge(ln_step, 1)
            nc.gpsimd.affine_select(out=ident[:], in_=ident[:], compare_op=ALU.not_equal, fill=1.0, base=0,
                                    pattern=[[-1, P]], channel_multiplier=1).then_inc(ident_ready, 1)
            nc.gpsimd.memset(minus_half[:], -0.5).then_inc(ln_step, 1)
            pool.wait_ge(ln_step, 2)
            pool.wait_ge(consts_in, 16 * 4)

            def clip(g):
                for t in range(QT):
                    count = at(pool, 16 * (g + 1))
                    pool.wait_ge(consts_in, 16 * 4)
                    pool.wait_ge(adj_loaded[t], count)
                    nc.gpsimd.tensor_scalar(adj_in[t][:], adj_in[t][:], ADJ_MIN, None, ALU.max).then_inc(adj_clipped, 1)

            clip(0)

            def layer_norm(g, first):
                steps = 4
                base = 2 + steps * g
                count = at(pool, QT * g + QT)
                pool.wait_ge(consts_in, 16 * 4)
                pool.wait_ge(stats_ready, count)
                nc.gpsimd.tensor_scalar(rstd[:, 0, :], mean_var[:, :, 1], LN_EPS, None, ALU.add).then_inc(ln_step, 1)
                pool.wait_ge(ln_step, base + 1)
                nc.gpsimd.tensor_tensor(rstd[:, 1, :], rstd[:, 0, :], minus_half[:], ALU.pow).then_inc(ln_step, 1)
                if not first:
                    pool.wait_ge(out_stored, 16 * g)
                count = at(pool, base + 2)
                pool.wait_ge(consts_in, 16 * 4)
                pool.wait_ge(ln_step, count)
                for t in range(QT):
                    ins = nc.gpsimd.tensor_scalar(normed[:, t, :], resid[:, t, :], mean_var[:, t, 0:1], rstd[:, 1, t:t + 1],
                                                  ALU.subtract, ALU.mult)
                ins.then_inc(ln_step, 1)
                pool.wait_ge(ln_step, base + 3)
                nc.gpsimd.tensor_tensor(normed[:], normed[:], gamma_row[:].unsqueeze(1).broadcast_to([P, QT, D]),
                                        ALU.mult).then_inc(ln_step, 1)
                pool.wait_ge(ln_step, base + 4)
                nc.gpsimd.tensor_tensor(normed[:], normed[:], beta_row[:].unsqueeze(1).broadcast_to([P, QT, D]),
                                        ALU.add).then_inc(normed_ready, 1)

            def widen(g, quad):
                count = at(pool, QUADS * g + quad + 1)
                pool.wait_ge(consts_in, 16 * 4)
                pool.wait_ge(inv_ready, count)
                nc.gpsimd.tensor_copy(inv_wide[quad][:], inv_sum[quad][:].unsqueeze(3)
                                      .broadcast_to([P, QT, QH, DK])).then_inc(inv_widened, 1)

            def attend(g, has_prev, has_cur, has_next):
                if has_next:
                    clip(g + 1)
                if has_cur:
                    widen(g, 0)
                if has_cur:
                    pool.wait_ge(x_loaded, 16 * (g + 1))
                    nc.gpsimd.tensor_tensor(x_bo[:], x_bo[:], bo_row[:].unsqueeze(1).broadcast_to([P, QT, D]),
                                            ALU.add).then_inc(x_bo_ready, 1)
                    widen(g, 1)
                if has_prev:
                    layer_norm(g - 1, isinstance(g, int) and g == 1)

            over_pairs(pool, attend)


def kernel(x, adj, L0_gnn_Wq, L0_gnn_bq, L0_gnn_Wk, L0_gnn_bk, L0_gnn_Wv, L0_gnn_bv, L0_gnn_Wo, L0_gnn_bo,
           L0_gnn_gamma, L0_gnn_beta):
    import numpy as np
    import concourse.bacc as bacc
    from concourse.bass_utils import run_bass_kernel_spmd

    nc = bacc.Bacc("TRN2", target_bir_lowering=False, num_devices=1)
    arrays = {
        "x": x, "xT": np.swapaxes(x, 1, 2), "adj": adj,
        "wqT": np.transpose(L0_gnn_Wq), "wkT": np.transpose(L0_gnn_Wk),
        "wvT": np.transpose(L0_gnn_Wv), "woT": np.transpose(L0_gnn_Wo),
        "bq": np.transpose(np.reshape(L0_gnn_bq, (DC, P))), "bk": np.transpose(np.reshape(L0_gnn_bk, (DC, P))), "bv": L0_gnn_bv, "bo": L0_gnn_bo,
        "gamma": L0_gnn_gamma, "beta": L0_gnn_beta,
    }
    arrays = {name: np.ascontiguousarray(a) for name, a in arrays.items()}
    args = {name: nc.dram_tensor(name, a.shape, mybir.dt.from_np(a.dtype), kind="ExternalInput").ap()
            for name, a in arrays.items()}
    out = nc.dram_tensor("out", x.shape, F32, kind="ExternalOutput").ap()
    graph_attention(nc, out=out, **args)
    r = run_bass_kernel_spmd(nc, [arrays], core_ids=[0])
    return r.results[0]["out"]
```

```python
from contextlib import ExitStack

import concourse.bass as bass
from concourse import mybir

F32 = mybir.dt.float32
F32R = mybir.dt.float32r
ALU = mybir.AluOpType
ACT = mybir.ActivationFunctionType

P = 128
B, N, D, H = 8, 1024, 256, 8
DK = D // H
DC = D // P
SCALE = float(DK) ** -0.5
LN_EPS = 1e-05
ADJ_MIN = 1e-08
NEVER = 3.0e38

HALVES = 2
TOK = N // HALVES
TT = TOK // P
OUTS = 6

QT = 2
PAIR = QT * P
PAIRS = B * N // PAIR
PPB = N // PAIR
UNITS = H * QT
QUADS = 2
QH = H // QUADS
KT = N // P
HK = KT // 2
AHEAD = 3
EXP_AHEAD = 2
LSLOTS = 4
LOG_STEPS = (11, 14)
GROUPS = P // DK

K_PART = [0, 1, 0, 1]
Q_PART = [0, 0, 1, 1]

HALF = UNITS // QUADS
PV_STEPS = {1: (0,), 2: (1,), 3: (2,), 4: (3, 4), 5: (5,), 6: (6,), 7: (7,)}
INV_STEP = 5
OUT_STEP = 10
STATS_STEPS = (12, 13)
PROJ_STEPS = (6, 8, 15)
OUTS_PAIR = len(PROJ_STEPS)
SPLIT_STEP = 3
assert OUTS_PAIR * PPB == OUTS * HALVES

RING = 3
USES = []
for _j in range(UNITS):
    USES.append(("a", _j))
    if _j % HALF == INV_STEP:
        USES.append(("inv", 1 - _j // HALF))
    if _j - OUT_STEP in range(QT):
        USES.append(("out", _j - OUT_STEP))
    if _j in PROJ_STEPS:
        USES.append(("proj", PROJ_STEPS.index(_j)))
    USES.append(("b", _j))
assert len(USES) % RING == 0 and (USES.index(("out", 1)) - USES.index(("out", 0))) == RING
SCALAR_TAKES_A = (0, 7, 9)


def unit(j):
    return 2 * (j // 4) + j % 2, (j % 4) // 2


def evacuator(use):
    return "vector" if use[0] == "a" and use[1] not in SCALAR_TAKES_A else "scalar"


def evacuated(use, engine):
    return sum(x[0] in "ab" and evacuator(x) == engine for x in USES[:USES.index(use) + 1])


VECTOR_EVACS = evacuated(USES[-1], "vector")
SCALAR_EVACS = evacuated(USES[-1], "scalar")


def bank_of(use):
    return USES.index(use) % RING


def graph_attention(nc, x, xT, adj, wqT, wkT, wvT, woT, bq, bk, bv, bo, gamma, beta, out):
    x_rows = x.rearrange("b t d -> (b t) d")
    adj_rows = adj.rearrange("b q k -> (b q) k")
    out_rows = out.rearrange("b t d -> (b t) d")
    q_dram = nc.dram_tensor("q_parts", (2 * D, B * N), F32, kind="Internal").ap()
    k_dram = nc.dram_tensor("k_parts", (2 * D, B * N), F32, kind="Internal").ap()
    v_dram = nc.dram_tensor("v_scratch", (B * N, D), F32, kind="Internal").ap()
    q_store = q_dram.rearrange("(l m p) t -> p m l t", l=2, m=DC)
    k_store = k_dram.rearrange("(l m p) t -> p m l t", l=2, m=DC)

    with ExitStack() as ctx:
        def sb(name, shape, dt=F32, scope=ctx):
            return scope.enter_context(nc.sbuf_tensor(name, shape, dt))

        def sem(name):
            return ctx.enter_context(nc.semaphore(name))

        ident = sb("ident", [P, P])
        bq_col = sb("bq_col", [P, DC])
        bqs_col = sb("bqs_col", [P, DC])
        bk_col = sb("bk_col", [P, DC])
        bv_row = sb("bv_row", [P, D])
        bo_row = sb("bo_row", [P, D])
        gamma_row = sb("gamma_row", [P, D])
        beta_row = sb("beta_row", [P, D])
        wo = sb("wo", [P, DC, D])
        minus_half = sb("minus_half", [P, QT])
        k_stack = sb("k_stack", [P, H, N], F32R)
        q_stack = [sb(f"q_stack{q}", [P, QH, PAIR], F32R) for q in range(QUADS)]
        v_sb = sb("v_sb", [P, QUADS, KT, P])
        w_hi = [sb(f"w_hi{i}", [P, DC, D], F32R) for i in range(3)]
        w_lo = [sb(f"w_lo{i}", [P, DC, D], F32R) for i in range(3)]
        x_raw = sb("x_raw", [P, DC, TOK])
        x_hi = [sb(f"x_hi{h}", [P, DC, TOK], F32R) for h in range(HALVES)]
        x_lo = [sb(f"x_lo{h}", [P, DC, TOK], F32R) for h in range(HALVES)]
        proj_out = [sb(f"proj_out{s}", [P, 2, TOK], F32R) for s in range(2)]
        adj_in = [sb(f"adj_in{t}", [P, N]) for t in range(QT)]
        log_adj = [sb(f"log_adj{t}", [P, N]) for t in range(QT)]
        neg_logits = [sb(f"neg_logits{s}", [P, N]) for s in range(LSLOTS)]
        neg_max = [sb(f"neg_max{s}", [P, 1]) for s in range(LSLOTS)]
        row_sum = [sb(f"row_sum{q}", [P, QT, QH]) for q in range(QUADS)]
        inv_sum = [sb(f"inv_sum{q}", [P, QT, QH]) for q in range(QUADS)]
        inv_wide = [sb(f"inv_wide{q}", [P, QT, QH, DK]) for q in range(QUADS)]
        inv_bcast = [sb(f"inv_bcast{q}", [P, PAIR]) for q in range(QUADS)]
        attn_T = [sb(f"attn_T{q}", [P, PAIR]) for q in range(QUADS)]
        x_bo = sb("x_bo", [P, QT, D])
        resid = sb("resid", [P, QT, D])
        stats = sb("stats", [P, QT, 6])
        mean_var = sb("mean_var", [P, QT, 2])
        rstd = sb("rstd", [P, 2, QT])
        normed = sb("normed", [P, QT, D])

        with ExitStack() as early:
            w_raw = [sb(f"w_raw{i}", [P, DC, D], F32, early) for i in range(3)]
            x_raw1 = sb("x_raw1", [P, DC, TOK], F32, early)
            k_out = [sb(f"k_out{h}", [P, DC, 2, TOK], F32R, early) for h in range(HALVES)]
            q_out = [sb(f"q_out{h}", [P, DC, 2, TOK], F32R, early) for h in range(HALVES)]
        probs_T = [sb(f"probs_T{q}", [P, QH, KT, PAIR]) for q in range(QUADS)]

        with nc.psum_tensor("proj", [P, OUTS, TOK], F32) as proj:
            pass
        score = [ctx.enter_context(nc.psum_tensor(f"score{s}", [P, N], F32)) for s in range(2)]
        ring = [ctx.enter_context(nc.psum_tensor(f"ring{s}", [P, TOK], F32)) for s in range(RING)]
        attn = ctx.enter_context(nc.psum_tensor("attn", [P, TOK], F32))

        weights_in = [sem(f"weights_in_{n}") for n in "kqv"]
        biases_in = sem("biases_in")
        consts_in = sem("consts_in")
        ident_ready = sem("ident_ready")
        bias_scaled = sem("bias_scaled")
        w_hi_ready = sem("w_hi_ready")
        w_lo_ready = sem("w_lo_ready")
        xT_loaded = [sem(f"xT_loaded{h}") for h in range(HALVES)]
        x_hi_ready = sem("x_hi_ready")
        x_lo_ready = sem("x_lo_ready")
        proj_ready = sem("proj_ready")
        proj_hi_done = sem("proj_hi_done")
        proj_done = sem("proj_done")
        first_stored = sem("first_stored")
        stored = [sem(f"stored{s}") for s in range(2)]

        k_loaded = [sem(f"k_loaded{i}") for i in range(H // 2)]
        q_loaded = [sem(f"q_loaded{q}") for q in range(QUADS)]
        v_loaded = [sem(f"v_loaded{q}") for q in range(QUADS)]
        adj_loaded = [sem(f"adj_loaded{t}") for t in range(QT)]
        x_loaded = sem("x_loaded")
        adj_clipped = sem("adj_clipped")
        log_adj_ready = sem("log_adj_ready")
        scores_ready = sem("scores_ready")
        logits_ready = sem("logits_ready")
        probs_ready = sem("probs_ready")
        half_a_ready = sem("half_a_ready")
        half_b_ready = sem("half_b_ready")
        vector_evac = sem("vector_evac")
        scalar_evac = sem("scalar_evac")
        inv_ready = sem("inv_ready")
        inv_widened = sem("inv_widened")
        pv_done = sem("pv_done")
        inv_broadcast = sem("inv_broadcast")
        inv_copied = sem("inv_copied")
        attn_ready = sem("attn_ready")
        out_proj_ready = sem("out_proj_ready")
        x_bo_ready = sem("x_bo_ready")
        resid_ready = sem("resid_ready")
        bn_step = sem("bn_step")
        stats_ready = sem("stats_ready")
        ln_step = sem("ln_step")
        normed_ready = sem("normed_ready")
        out_stored = sem("out_stored")

        def over_pairs(eng, body):
            def batch(b, first, last):
                for i in range(PPB):
                    body(PPB * b + i, b, i, not (first and i == 0), True, not (last and i == PPB - 1), not last)
            batch(0, True, False)
            with eng.Fori(1, B - 1) as b:
                batch(b, False, False)
            batch(B - 1, False, True)
            body(PAIRS, B, 0, True, False, False, False)

        def at(eng, value):
            return value if isinstance(value, int) else eng.to_reg(value)

        block = ctx.enter_context(nc.Block())

        @block.sync
        def _(sp):
            def load_weights(i, w):
                sp.dma_start(w_raw[i][:], w.rearrange("(c p) n -> p c n", p=P)).then_inc(weights_in[i], 16)

            def load_x(raw, b, h):
                sp.dma_start(raw[:], xT.rearrange("b (c p) t -> p b c t", p=P)
                             [:, bass.ds(b, 1), :, h * TOK:(h + 1) * TOK].rearrange("p o c t -> p (o c) t")).then_inc(xT_loaded[h], 16)

            load_weights(0, wkT)
            load_x(x_raw, 0, 0)
            load_weights(1, wqT)
            sp.dma_start(bk_col[:], bk).then_inc(biases_in, 16)
            sp.dma_start(bq_col[:], bq).then_inc(biases_in, 16)
            load_weights(2, wvT)
            sp.dma_start(bv_row[:], bv.partition_broadcast(P)).then_inc(biases_in, 16)
            load_x(x_raw1, 0, 1)
            for row, vec in ((bo_row, bo), (gamma_row, gamma), (beta_row, beta)):
                sp.dma_start(row[:], vec.partition_broadcast(P)).then_inc(consts_in, 16)
            sp.dma_start(wo[:], woT.rearrange("(c p) n -> p c n", p=P)).then_inc(consts_in, 16)

            def load_k(i, b):
                for gr in range(GROUPS):
                    row = K_PART[gr] * D + 2 * i * DK
                    sp.dma_start(k_stack[gr * DK:(gr + 1) * DK, 2 * i:2 * i + 2, :].bitcast(F32),
                                 k_dram[row:row + 2 * DK, bass.ds(b * N, N)]
                                 .rearrange("(h d) t -> d h t", h=2)).then_inc(k_loaded[i], 16)

            def load_q(q, g):
                for gr in range(GROUPS):
                    row = Q_PART[gr] * D + q * P
                    sp.dma_start(q_stack[q][gr * DK:(gr + 1) * DK, :, :].bitcast(F32),
                                 q_dram[row:row + P, bass.ds(g * PAIR, PAIR)]
                                 .rearrange("(h d) t -> d h t", h=QH)).then_inc(q_loaded[q], 16)

            def load_v(q, b):
                sp.dma_start(v_sb[:, q], v_dram[bass.ds(b * N, N), q * P:(q + 1) * P]
                             .rearrange("(k p) d -> p k d", p=P)).then_inc(v_loaded[q], 16)

            def load_adj(t, g):
                sp.dma_start(adj_in[t][:], adj_rows[bass.ds(g * PAIR + t * P, P), :]).then_inc(adj_loaded[t], 16)

            def store_first(dst, src, h, done):
                sp.wait_ge(proj_done, done)
                for m in range(DC):
                    sp.dma_start(dst[:, m, :, h * TOK:(h + 1) * TOK],
                                 src[h][:, m].bitcast(F32)).then_inc(first_stored, 16)

            load_adj(0, 0)
            load_adj(1, 0)
            sp.wait_ge(x_lo_ready, 1)
            load_x(x_raw, 1, 0)
            store_first(k_store, k_out, 0, 2)
            store_first(q_store, q_out, 0, 4)
            store_first(k_store, k_out, 1, 6)
            sp.wait_ge(first_stored, 16 * 6)
            load_k(0, 0)
            load_q(0, 0)
            store_first(q_store, q_out, 1, 8)
            load_k(1, 0)
            load_q(1, 0)
            load_k(2, 0)
            for t in range(QT):
                sp.wait_ge(log_adj_ready, t + 1)
                load_adj(t, 1)
            load_k(3, 0)
            sp.wait_ge(first_stored, 16 * 8)

            def store_projection(g, b, i, n):
                h, o = i // 2, OUTS_PAIR * (i % 2) + n
                count = at(sp, OUTS * (HALVES * (b + 1) + h) + o + 1)
                sp.wait_ge(weights_in[0], 16)
                sp.wait_ge(proj_done, count)
                token = (b + 1) * N + h * TOK
                if o < 4:
                    dst = (k_store if o < 2 else q_store)[:, o % DC, :, bass.ds(token, TOK)]
                    src = proj_out[o % 2][:].bitcast(F32)
                else:
                    dst = v_dram[bass.ds(token + (o - 4) * 2 * P, 2 * P), :].rearrange("(k p) d -> p k d", p=P)
                    src = proj_out[o % 2][:, 0, :].bitcast(F32).rearrange("p (k d) -> p k d", k=2)
                sp.dma_start(dst, src).then_inc(stored[o % 2], 16)

            def wait_stored(b, counts):
                for buf in range(2):
                    count = at(sp, 16 * (HALVES * 3 * b + counts[buf]))
                    sp.wait_ge(weights_in[0], 16)
                    sp.wait_ge(stored[buf], count)

            def attend(g, b, i, has_prev, has_cur, has_next, projecting):
                if not has_cur:
                    store_out(g - 2)
                    store_out(g - 1)
                    return
                last_of_batch = i == PPB - 1
                if projecting and i % 2 == 0 and not (isinstance(g, int) and g == 0):
                    h = i // 2
                    count = at(sp, HALVES * (b + 1) + h)
                    sp.wait_ge(weights_in[0], 16)
                    sp.wait_ge(x_lo_ready, count)
                    count = at(sp, OUTS * (HALVES * b + h + 1))
                    sp.wait_ge(weights_in[0], 16)
                    sp.wait_ge(proj_ready, count)
                    load_x(x_raw, b + 1, h)
                if i == 0 and has_prev:
                    wait_stored(b, (0, 0))
                    count = at(sp, QUADS * g - 1)
                    sp.wait_ge(weights_in[0], 16)
                    sp.wait_ge(pv_done, count)
                    load_v(0, b)
                if last_of_batch and has_next:
                    wait_stored(b, (5, 4))
                    count = at(sp, UNITS * g + 4)
                    sp.wait_ge(weights_in[0], 16)
                    sp.wait_ge(scores_ready, count)
                    load_k(0, b + 1)
                if has_next:
                    count = at(sp, UNITS * g + HALF)
                    sp.wait_ge(weights_in[0], 16)
                    sp.wait_ge(scores_ready, count)
                    load_q(0, g + 1)
                    if last_of_batch:
                        load_k(1, b + 1)
                if not (isinstance(g, int) and g < 2):
                    store_out(g - 2)
                if projecting:
                    store_projection(g, b, i, 0)
                if i == 0 and has_prev:
                    count = at(sp, QUADS * g)
                    sp.wait_ge(weights_in[0], 16)
                    sp.wait_ge(pv_done, count)
                    load_v(1, b)
                if last_of_batch and has_next:
                    count = at(sp, UNITS * g + 12)
                    sp.wait_ge(weights_in[0], 16)
                    sp.wait_ge(scores_ready, count)
                    load_k(2, b + 1)
                if projecting:
                    store_projection(g, b, i, 1)
                if has_prev:
                    count = at(sp, QT * g)
                    sp.wait_ge(weights_in[0], 16)
                    sp.wait_ge(resid_ready, count)
                sp.dma_start(x_bo[:], x_rows[bass.ds(g * PAIR, PAIR), :]
                             .rearrange("(s p) d -> p s d", p=P)).then_inc(x_loaded, 16)
                if has_next:
                    count = at(sp, UNITS * g + UNITS)
                    sp.wait_ge(weights_in[0], 16)
                    sp.wait_ge(scores_ready, count)
                    load_q(1, g + 1)
                    if last_of_batch:
                        load_k(3, b + 1)
                if projecting or i < PPB - 2:
                    for t in range(QT):
                        count = at(sp, QT * g + QT + t + 1)
                        sp.wait_ge(weights_in[0], 16)
                        sp.wait_ge(log_adj_ready, count)
                        load_adj(t, g + 2)
                if projecting:
                    store_projection(g, b, i, 2)

            def store_out(g):
                count = at(sp, g + 1)
                sp.wait_ge(weights_in[0], 16)
                sp.wait_ge(normed_ready, count)
                sp.dma_start(out_rows[bass.ds(g * PAIR, PAIR), :].rearrange("(s p) d -> p s d", p=P),
                             normed[:]).then_inc(out_stored, 16)

            over_pairs(sp, attend)
            sp.wait_ge(out_stored, 16 * PAIRS)

        @block.tensor
        def _(pe):
            def channel_projection(bank, h, o):
                w, m = o // 2, o % DC
                terms = [(wp, xp, c) for c in range(DC)
                         for wp, xp in ((w_hi, x_hi), (w_hi, x_lo), (w_lo, x_hi))]
                for s, (wp, xp, c) in enumerate(terms):
                    mm = nc.tensor.matmul(bank, wp[w][:, c, m * P:(m + 1) * P], xp[h][:, c, :],
                                          start=(s == 0), stop=(s == len(terms) - 1))
                mm.then_inc(proj_ready, 1)

            def value_projection(bank, h, o):
                for half in range(2):
                    t = 2 * (o - 4) + half
                    terms = [(xp, wp, c) for c in range(DC)
                             for xp, wp in ((x_hi, w_hi), (x_lo, w_hi), (x_hi, w_lo))]
                    for s, (xp, wp, c) in enumerate(terms):
                        mm = nc.tensor.matmul(bank[:, half * D:(half + 1) * D],
                                              xp[h][:, c, t * P:(t + 1) * P], wp[2][:, c, :],
                                              start=(s == 0), stop=(s == len(terms) - 1))
                mm.then_inc(proj_ready, 1)

            for h in range(HALVES):
                pe.wait_ge(x_hi_ready, h + 1)
                pe.wait_ge(x_lo_ready, h + 1)
                for o in range(4):
                    if h == 0:
                        pe.wait_ge(w_hi_ready, o // 2 + 1)
                        pe.wait_ge(w_lo_ready, o // 2 + 1)
                    else:
                        pe.wait_ge(proj_done, o + 1)
                    channel_projection(proj[:, o, :], h, o)
            pe.wait_ge(w_hi_ready, 3)
            pe.wait_ge(w_lo_ready, 3)
            for h in range(HALVES):
                for o in (4, 5):
                    if h == 1:
                        pe.wait_ge(proj_done, 8 + o - 3)
                    value_projection(proj[:, o, :], h, o)

            pe.wait_ge(proj_done, OUTS * HALVES)
            pe.wait_ge(ident_ready, 1)
            pe.wait_ge(consts_in, 16 * 4)

            def scores(g, b, j, first):
                head, t = unit(j)
                quad = j // HALF
                if j % HALF == 0:
                    pe.wait_ge(q_loaded[quad], 16 * GROUPS * (g + 1))
                if j % 4 == 0:
                    pe.wait_ge(k_loaded[j // 4], 16 * GROUPS * (b + 1))
                if not (first and j < 2):
                    pe.wait_ge(logits_ready, UNITS * g + j - 1)
                for n in range(2):
                    mm = nc.tensor.matmul(score[j % 2][:, n * TOK:(n + 1) * TOK],
                                          q_stack[quad][:, head % QH, t * P:(t + 1) * P],
                                          k_stack[:, head, n * TOK:(n + 1) * TOK], start=True, stop=True)
                mm.then_inc(scores_ready, 1)

            def ring_free(g, i, use, first, projecting):
                k = USES.index(use) - RING
                while not first or k >= 0:
                    before, pairs_back = USES[k % len(USES)], int(k < 0)
                    missing = (first and (before[0] == "out" or before == ("inv", 1))
                               or before[0] == "proj" and not projecting and not (i == 0 and pairs_back))
                    if not missing:
                        break
                    k -= RING
                else:
                    return
                if before[0] == "out":
                    pe.wait_ge(resid_ready, QT * (g - 1) + before[1] + 1)
                elif before[0] == "inv":
                    pe.wait_ge(inv_copied, QUADS * g + 1 - before[1])
                elif before[0] == "proj":
                    pe.wait_ge(proj_done, OUTS_PAIR * (g - pairs_back) + OUTS * HALVES + before[1] + 1)
                elif evacuator(before) == "vector":
                    pe.wait_ge(vector_evac, VECTOR_EVACS * (g - pairs_back) + evacuated(before, "vector"))
                else:
                    pe.wait_ge(scalar_evac, SCALAR_EVACS * (g - pairs_back) + evacuated(before, "scalar"))

            def transposes(g, j, half):
                bank = ring[bank_of(("ab"[half], j))]
                for k in range(HK):
                    kt = half * HK + k
                    mm = nc.tensor.transpose(bank[:, k * P:(k + 1) * P],
                                             neg_logits[j % LSLOTS][:, kt * P:(kt + 1) * P], ident[:])
                mm.then_inc(half_b_ready if half else half_a_ready, 1)

            def values(g, b, quad, kt):
                if kt in (0, HK):
                    last = ("b" if kt else "a", HALF * quad + HALF - 1)
                    pe.wait_ge(vector_evac, VECTOR_EVACS * g + evacuated(last, "vector"))
                    pe.wait_ge(scalar_evac, SCALAR_EVACS * g + evacuated(last, "scalar"))
                if kt == 0:
                    if not isinstance(b, int) or b > 0:
                        pe.wait_ge(v_loaded[quad], 16 * b)
                    if not (isinstance(g, int) and g == 0 and quad == 0):
                        pe.wait_ge(attn_ready, QUADS * g + quad)
                for hh in range(QH):
                    mm = nc.tensor.matmul(attn[hh * DK:(hh + 1) * DK, 0:PAIR],
                                          v_sb[:, quad, kt, hh * DK:(hh + 1) * DK],
                                          probs_T[quad][:, hh, kt, :], start=(kt == 0), stop=(kt == KT - 1))
                if kt == KT - 1:
                    mm.then_inc(pv_done, 1)

            def broadcast_inverse(g, quad):
                pe.wait_ge(inv_widened, QUADS * g + quad + 1)
                for t in range(QT):
                    mm = nc.tensor.transpose(ring[bank_of(("inv", quad))][:, t * P:(t + 1) * P],
                                             inv_wide[quad][:, t, :, :].rearrange("p h d -> p (h d)"), ident[:])
                mm.then_inc(inv_broadcast, 1)

            def output_projection(g, t):
                if t == 0:
                    pe.wait_ge(attn_ready, QUADS * g + QUADS)
                for quad in range(QUADS):
                    mm = nc.tensor.matmul(ring[bank_of(("out", t))][:, 0:D], attn_T[quad][:, t * P:(t + 1) * P],
                                          wo[:, quad, :], start=(quad == 0), stop=(quad == QUADS - 1))
                mm.then_inc(out_proj_ready, 1)

            for j in range(AHEAD):
                scores(0, 0, j, True)

            def attend(g, b, i, has_prev, has_cur, has_next, projecting):
                first = not has_prev

                def free(use):
                    ring_free(g, i, use, first, projecting)

                if not has_cur:
                    pe.wait_ge(vector_evac, VECTOR_EVACS * g)
                    pe.wait_ge(scalar_evac, SCALAR_EVACS * g)
                for j in range(UNITS):
                    if has_cur:
                        if j + AHEAD < UNITS:
                            scores(g, b, j + AHEAD, first)
                        elif has_next:
                            scores(g + 1, b + 1 if i == PPB - 1 else b, j + AHEAD - UNITS, False)
                        pe.wait_ge(probs_ready, UNITS * g + j + 1)
                        free(("a", j))
                        transposes(g, j, 0)
                    for kt in PV_STEPS.get(j % HALF, ()):
                        if j < HALF and has_prev:
                            values(g - 1, b - 1 if i == 0 else b, 1, kt)
                        if j >= HALF and has_cur:
                            values(g, b, 0, kt)
                    if j == INV_STEP and has_prev:
                        if has_cur:
                            free(("inv", 1))
                        broadcast_inverse(g - 1, 1)
                    if j == HALF + INV_STEP and has_cur:
                        free(("inv", 0))
                        broadcast_inverse(g, 0)
                    if j - OUT_STEP in range(QT) and has_prev:
                        if has_cur or j > OUT_STEP:
                            free(("out", j - OUT_STEP))
                        output_projection(g - 1, j - OUT_STEP)
                    if j in PROJ_STEPS and projecting:
                        n = PROJ_STEPS.index(j)
                        h, o = i // 2, OUTS_PAIR * (i % 2) + n
                        if o == 0:
                            pe.wait_ge(x_hi_ready, HALVES * (b + 1) + h + 1)
                            pe.wait_ge(x_lo_ready, HALVES * (b + 1) + h + 1)
                        free(("proj", n))
                        (channel_projection if o < 4 else value_projection)(ring[bank_of(("proj", n))][:, :], h, o)
                    if has_cur:
                        free(("b", j))
                        transposes(g, j, 1)

            over_pairs(pe, attend)

        @block.scalar
        def _(act):
            nc.scalar.preload_act_table_set("natural_log_exp_and_others")

            def split_weights(i):
                act.wait_ge(weights_in[i], 16)
                nc.scalar.activation(w_hi[i][:], w_raw[i][:], ACT.Copy,
                                     scale=SCALE if i == 1 else 1.0).then_inc(w_hi_ready, 1)

            def split_x(raw, b, h):
                act.wait_ge(xT_loaded[h], 16 * (b + 1))
                nc.scalar.activation(x_hi[h][:], raw[:], ACT.Copy).then_inc(x_hi_ready, 1)

            split_weights(0)
            split_x(x_raw, 0, 0)
            split_weights(1)
            split_weights(2)
            act.wait_ge(biases_in, 16 * 3)
            act.wait_ge(bias_scaled, 1)

            split_x(x_raw1, 0, 1)

            def high_part(dst, bank, ready, o):
                act.wait_ge(proj_ready, ready)
                nc.scalar.activation(dst, bank, ACT.Identity,
                                     bias=(bk_col if o < 2 else bqs_col)[:, o % DC:o % DC + 1]).then_inc(proj_hi_done, 1)

            for h in range(HALVES):
                for o in range(4):
                    high_part((k_out if o < 2 else q_out)[h][:, o % DC, 0, :], proj[:, o, :], 4 * h + o + 1, o)

            def log_adjacency(g, t):
                act.wait_ge(adj_clipped, QT * g + t + 1)
                nc.scalar.activation(log_adj[t][:], adj_in[t][:], ACT.Ln).then_inc(log_adj_ready, 1)

            def exponential(g, j):
                head, t = unit(j)
                act.wait_ge(logits_ready, UNITS * g + j + 1)
                nc.scalar.activation(neg_logits[j % LSLOTS][:], neg_logits[j % LSLOTS][:], ACT.Exp,
                                     bias=neg_max[j % LSLOTS][:], scale=-1.0,
                                     accum_out=row_sum[j // HALF][:, t, head % QH:head % QH + 1]
                                     ).then_inc(probs_ready, 1)

            for j in range(EXP_AHEAD):
                log_adjacency(0, j)
                exponential(0, j)

            def copy_inverse(g, quad):
                act.wait_ge(inv_broadcast, QUADS * g + quad + 1)
                nc.scalar.copy(inv_bcast[quad][:], ring[bank_of(("inv", quad))][:, 0:PAIR]).then_inc(inv_copied, 1)

            def attend(g, b, i, has_prev, has_cur, has_next, projecting):
                for j in range(UNITS):
                    if has_next and j in LOG_STEPS:
                        t = LOG_STEPS.index(j)
                        act.wait_ge(logits_ready, UNITS * g + 14 + 2 * t)
                        log_adjacency(g + 1, t)
                    if has_cur:
                        if j + EXP_AHEAD < UNITS:
                            exponential(g, j + EXP_AHEAD)
                        elif has_next:
                            exponential(g + 1, j + EXP_AHEAD - UNITS)
                        head, t = unit(j)
                        if j == 0 and not has_prev:
                            act.wait_ge(first_stored, 16 * 8)
                        if j % HALF == 0 and has_prev:
                            act.wait_ge(pv_done, QUADS * g + j // HALF - 1)
                    if projecting and i % 2 == 0 and j == SPLIT_STEP:
                        split_x(x_raw, b + 1, i // 2)
                    for half in range(2):
                        if half == 1 and j == INV_STEP and has_prev:
                            copy_inverse(g - 1, 1)
                        if half == 1 and j == HALF + INV_STEP and has_cur:
                            copy_inverse(g, 0)
                        if half == 1 and j in PROJ_STEPS and projecting:
                            n = PROJ_STEPS.index(j)
                            h, o = i // 2, OUTS_PAIR * (i % 2) + n
                            if o < 4:
                                if not (isinstance(b, int) and b == 0 and i == 0 and o < 2):
                                    act.wait_ge(stored[o % 2], 16 * (3 * (HALVES * b + h) + o // 2))
                                high_part(proj_out[o % 2][:, 0, :], ring[bank_of(("proj", n))][:, :],
                                          OUTS * (HALVES * (b + 1) + h) + o + 1, o)
                        use = ("ab"[half], j)
                        if has_cur and evacuator(use) == "scalar":
                            act.wait_ge(half_b_ready if half else half_a_ready, UNITS * g + j + 1)
                            nc.scalar.copy(probs_T[j // HALF][:, head % QH, half * HK:(half + 1) * HK, t * P:(t + 1) * P],
                                           ring[bank_of(use)][:, :].rearrange("p (k q) -> p k q", k=HK)
                                           ).then_inc(scalar_evac, 1)

            over_pairs(act, attend)

        @block.vector
        def _(dve):
            def split_weights(i):
                dve.wait_ge(w_hi_ready, i + 1)
                nc.vector.scalar_tensor_tensor(w_lo[i][:], w_raw[i][:], SCALE if i == 1 else 1.0,
                                               w_hi[i][:].bitcast(F32), ALU.mult, ALU.subtract).then_inc(w_lo_ready, 1)

            def split_x(raw, b, h):
                n = HALVES * b + h
                dve.wait_ge(x_hi_ready, n + 1)
                nc.vector.tensor_tensor(x_lo[h][:], raw[:], x_hi[h][:].bitcast(F32),
                                        ALU.subtract).then_inc(x_lo_ready, 1)

            split_weights(0)
            split_x(x_raw, 0, 0)
            split_weights(1)
            split_weights(2)
            dve.wait_ge(biases_in, 16 * 3)
            nc.vector.tensor_scalar(bqs_col[:], bq_col[:], SCALE, None, ALU.mult).then_inc(bias_scaled, 1)
            dve.wait_ge(bias_scaled, 1)

            split_x(x_raw1, 0, 1)

            def low_part(dst, hi, bank, n, o):
                dve.wait_ge(proj_hi_done, 4 * n + o + 1)
                nc.vector.scalar_tensor_tensor(dst, bank, (bk_col if o < 2 else bqs_col)[:, o % DC:o % DC + 1],
                                               hi.bitcast(F32), ALU.add, ALU.subtract).then_inc(proj_done, 1)

            def values_out(dst, bank, ready):
                dve.wait_ge(proj_ready, ready)
                nc.vector.tensor_tensor(dst, bank.rearrange("p (s q d) -> p s q d", s=2, q=QUADS),
                                        bv_row[:].rearrange("p (q d) -> p q d", q=QUADS).unsqueeze(1)
                                        .broadcast_to([P, 2, QUADS, P]), ALU.add).then_inc(proj_done, 1)

            for h in range(HALVES):
                for o in range(4):
                    dst = (k_out if o < 2 else q_out)[h]
                    low_part(dst[:, o % DC, 1, :], dst[:, o % DC, 0, :], proj[:, o, :], h, o)
            for h in range(HALVES):
                for o in (4, 5):
                    kt = TT * h + 2 * (o - 4)
                    values_out(v_sb[:, :, kt:kt + 2, :].rearrange("p q s d -> p s q d"), proj[:, o, :], 8 + 2 * h + o - 3)

            def logits(g, j):
                head, t = unit(j)
                if j in (0, 2):
                    dve.wait_ge(log_adj_ready, QT * g + t + 1)
                count = at(dve, UNITS * g + j + 1)
                dve.wait_ge(bias_scaled, 1)
                dve.wait_ge(scores_ready, count)
                nc.vector.tensor_tensor_reduce(neg_logits[j % LSLOTS][:], score[j % 2][:], log_adj[t][:], -1.0,
                                               NEVER, ALU.add, ALU.min,
                                               neg_max[j % LSLOTS][:]).then_inc(logits_ready, 1)

            for j in range(AHEAD):
                logits(0, j)

            def inverse(g, quad):
                dve.wait_ge(probs_ready, UNITS * g + HALF * quad + HALF)
                nc.vector.reciprocal(inv_sum[quad][:], row_sum[quad][:]).then_inc(inv_ready, 1)

            def normalise(g, quad):
                dve.wait_ge(pv_done, QUADS * g + quad + 1)
                dve.wait_ge(inv_copied, QUADS * g + quad + 1)
                nc.vector.tensor_tensor(attn_T[quad][:], attn[:, 0:PAIR], inv_bcast[quad][:],
                                        ALU.mult).then_inc(attn_ready, 1)

            def residual(g, t, first):
                dve.wait_ge(out_proj_ready, QT * g + t + 1)
                if t == 0:
                    dve.wait_ge(x_bo_ready, g + 1)
                    if not first:
                        dve.wait_ge(normed_ready, g)
                nc.vector.tensor_tensor(resid[:, t, :], ring[bank_of(("out", t))][:, 0:D], x_bo[:, t, :],
                                        ALU.add).then_inc(resid_ready, 1)

            def statistics(g, t):
                dve.wait_ge(resid_ready, QT * g + t + 1)
                nc.vector.bn_stats(stats[:, t, :], resid[:, t, :]).then_inc(bn_step, 1)

            def mean_variance(g):
                count = at(dve, QT * g + QT)
                dve.wait_ge(bias_scaled, 1)
                dve.wait_ge(bn_step, count)
                for t in range(QT):
                    nc.vector.bn_aggr(mean_var[:, t, :], stats[:, t, :]).then_inc(stats_ready, 1)

            def attend(g, b, i, has_prev, has_cur, has_next, projecting):
                for j in range(UNITS):
                    if j % HALF == 0 and has_prev:
                        normalise(g - 1, j // HALF)
                    if has_cur:
                        head, t = unit(j)
                        for half in range(2):
                            use = ("ab"[half], j)
                            if j == 0 and not has_prev and half == 0:
                                dve.wait_ge(first_stored, 16 * 8)
                            if j % HALF == 0 and has_prev and half == 0:
                                dve.wait_ge(pv_done, QUADS * g + j // HALF - 1)
                            if evacuator(use) == "vector":
                                dve.wait_ge(half_b_ready if half else half_a_ready, UNITS * g + j + 1)
                                nc.vector.tensor_copy(probs_T[j // HALF][:, head % QH, half * HK:(half + 1) * HK, t * P:(t + 1) * P],
                                                      ring[bank_of(use)][:, :].rearrange("p (k q) -> p k q", k=HK)
                                                      ).then_inc(vector_evac, 1)
                    if has_cur:
                        if j + AHEAD < UNITS:
                            logits(g, j + AHEAD)
                        elif has_next:
                            logits(g + 1, j + AHEAD - UNITS)
                    if projecting and i % 2 == 0 and j == SPLIT_STEP:
                        split_x(x_raw, b + 1, i // 2)
                    if j in PROJ_STEPS and projecting:
                        n = PROJ_STEPS.index(j)
                        h, o = i // 2, OUTS_PAIR * (i % 2) + n
                        buf, bank = proj_out[o % 2], ring[bank_of(("proj", n))][:, :]
                        if o < 4:
                            low_part(buf[:, 1, :], buf[:, 0, :], bank, HALVES * (b + 1) + h, o)
                        else:
                            dve.wait_ge(stored[o % 2], 16 * (3 * (HALVES * b + h) + o // 2))
                            values_out(buf[:, 0, :].bitcast(F32).rearrange("p (s q d) -> p s q d", s=2, q=QUADS),
                                       bank, OUTS * (HALVES * (b + 1) + h) + o + 1)
                    if j % HALF == HALF - 1 and has_cur:
                        inverse(g, j // HALF)
                    if j - OUT_STEP in range(QT) and has_prev:
                        residual(g - 1, j - OUT_STEP, isinstance(g, int) and g == 1)
                    if j in STATS_STEPS and has_prev:
                        statistics(g - 1, STATS_STEPS.index(j))
                    if j == STATS_STEPS[-1] + 1 and has_prev:
                        mean_variance(g - 1)

            over_pairs(dve, attend)

        @block.gpsimd
        def _(pool):
            nc.gpsimd.memset(ident[:], 0.0).then_inc(ln_step, 1)
            pool.wait_ge(ln_step, 1)
            nc.gpsimd.affine_select(out=ident[:], in_=ident[:], compare_op=ALU.not_equal, fill=1.0, base=0,
                                    pattern=[[-1, P]], channel_multiplier=1).then_inc(ident_ready, 1)
            nc.gpsimd.memset(minus_half[:], -0.5).then_inc(ln_step, 1)
            pool.wait_ge(ln_step, 2)
            pool.wait_ge(consts_in, 16 * 4)

            def clip(g):
                for t in range(QT):
                    count = at(pool, 16 * (g + 1))
                    pool.wait_ge(consts_in, 16 * 4)
                    pool.wait_ge(adj_loaded[t], count)
                    nc.gpsimd.tensor_scalar(adj_in[t][:], adj_in[t][:], ADJ_MIN, None, ALU.max).then_inc(adj_clipped, 1)

            clip(0)

            def layer_norm(g, first):
                steps = 4
                base = 2 + steps * g
                count = at(pool, QT * g + QT)
                pool.wait_ge(consts_in, 16 * 4)
                pool.wait_ge(stats_ready, count)
                nc.gpsimd.tensor_scalar(rstd[:, 0, :], mean_var[:, :, 1], LN_EPS, None, ALU.add).then_inc(ln_step, 1)
                pool.wait_ge(ln_step, base + 1)
                nc.gpsimd.tensor_tensor(rstd[:, 1, :], rstd[:, 0, :], minus_half[:], ALU.pow).then_inc(ln_step, 1)
                if not first:
                    pool.wait_ge(out_stored, 16 * g)
                count = at(pool, base + 2)
                pool.wait_ge(consts_in, 16 * 4)
                pool.wait_ge(ln_step, count)
                for t in range(QT):
                    ins = nc.gpsimd.tensor_scalar(normed[:, t, :], resid[:, t, :], mean_var[:, t, 0:1], rstd[:, 1, t:t + 1],
                                                  ALU.subtract, ALU.mult)
                ins.then_inc(ln_step, 1)
                pool.wait_ge(ln_step, base + 3)
                nc.gpsimd.tensor_tensor(normed[:], normed[:], gamma_row[:].unsqueeze(1).broadcast_to([P, QT, D]),
                                        ALU.mult).then_inc(ln_step, 1)
                pool.wait_ge(ln_step, base + 4)
                nc.gpsimd.tensor_tensor(normed[:], normed[:], beta_row[:].unsqueeze(1).broadcast_to([P, QT, D]),
                                        ALU.add).then_inc(normed_ready, 1)

            def widen(g, quad):
                count = at(pool, QUADS * g + quad + 1)
                pool.wait_ge(consts_in, 16 * 4)
                pool.wait_ge(inv_ready, count)
                nc.gpsimd.tensor_copy(inv_wide[quad][:], inv_sum[quad][:].unsqueeze(3)
                                      .broadcast_to([P, QT, QH, DK])).then_inc(inv_widened, 1)

            def attend(g, b, i, has_prev, has_cur, has_next, projecting):
                if has_next:
                    clip(g + 1)
                if has_cur:
                    widen(g, 0)
                if has_cur:
                    pool.wait_ge(x_loaded, 16 * (g + 1))
                    nc.gpsimd.tensor_tensor(x_bo[:], x_bo[:], bo_row[:].unsqueeze(1).broadcast_to([P, QT, D]),
                                            ALU.add).then_inc(x_bo_ready, 1)
                    widen(g, 1)
                if has_prev:
                    layer_norm(g - 1, isinstance(g, int) and g == 1)

            over_pairs(pool, attend)


def kernel(x, adj, L0_gnn_Wq, L0_gnn_bq, L0_gnn_Wk, L0_gnn_bk, L0_gnn_Wv, L0_gnn_bv, L0_gnn_Wo, L0_gnn_bo,
           L0_gnn_gamma, L0_gnn_beta):
    import numpy as np
    import concourse.bacc as bacc
    from concourse.bass_utils import run_bass_kernel_spmd

    nc = bacc.Bacc("TRN2", target_bir_lowering=False, num_devices=1)
    arrays = {
        "x": x, "xT": np.swapaxes(x, 1, 2), "adj": adj,
        "wqT": np.transpose(L0_gnn_Wq), "wkT": np.transpose(L0_gnn_Wk),
        "wvT": np.transpose(L0_gnn_Wv), "woT": np.transpose(L0_gnn_Wo),
        "bq": np.transpose(np.reshape(L0_gnn_bq, (DC, P))), "bk": np.transpose(np.reshape(L0_gnn_bk, (DC, P))), "bv": L0_gnn_bv, "bo": L0_gnn_bo,
        "gamma": L0_gnn_gamma, "beta": L0_gnn_beta,
    }
    arrays = {name: np.ascontiguousarray(a) for name, a in arrays.items()}
    args = {name: nc.dram_tensor(name, a.shape, mybir.dt.from_np(a.dtype), kind="ExternalInput").ap()
            for name, a in arrays.items()}
    out = nc.dram_tensor("out", x.shape, F32, kind="ExternalOutput").ap()
    graph_attention(nc, out=out, **args)
    r = run_bass_kernel_spmd(nc, [arrays], core_ids=[0])
    return r.results[0]["out"]
```
